# Optimizing a Trainium2 kernel written in Bass

```python
import numpy as np
import jax
import jax.numpy as jnp

def _softmax(x, axis=-1):
    return jax.nn.softmax(x, axis=axis)

def _gelu(x):
    return jax.nn.gelu(x, approximate=True)

def _silu(x):
    return jax.nn.silu(x)

def _sigmoid(x):
    return jax.nn.sigmoid(x)

def _layernorm(x, axis=-1, eps=1e-05):
    m = jnp.mean(x, axis=axis, keepdims=True)
    v = jnp.var(x, axis=axis, keepdims=True)
    return (x - m) / jnp.sqrt(v + eps)

def _scatter_add(tgt, idx, src, axis=0):
    return tgt.at[idx].add(src)

def _segment_sum(src, seg, n):
    return jax.ops.segment_sum(src, seg, n)
kernel_name = 'mk_xattn_seq_d2_seqx_r4_a3666f'

def setup_inputs(seed: int=0):
    np.random.seed(seed)
    _w = jnp.asarray

    def _rec_inputs():
        import jax
        import jax.numpy as jnp
        _rk = jax.random.key(seed)
        x = -0.0002928 + 1 * jax.random.normal(jax.random.fold_in(_rk, 1), (32, 128, 512), jnp.float32)
        _lenS = 128 - jax.random.randint(jax.random.fold_in(_rk, 7), (32,), 0, max(1, 128 // 4) + 1, jnp.int32)
        _lenS2 = 128 - jax.random.randint(jax.random.fold_in(_rk, 8), (32,), 0, max(1, 128 // 4) + 1, jnp.int32)
        _ctx_2048P = jax.random.normal(jax.random.fold_in(_rk, 11), (32, 16, 512), jnp.float32)
        _ctx_2048c = jax.random.dirichlet(jax.random.fold_in(_rk, 511), 0.3 * jnp.ones((16,), jnp.float32), (32, 128))
        _ctx_2048t = jnp.einsum('bsk,bkd->bsd', _ctx_2048c, _ctx_2048P)
        _ctx_2048t = _ctx_2048t * jax.lax.rsqrt(jnp.mean(jnp.square(_ctx_2048t)) + 1e-12) * 0.953939
        ctx_2048 = -1.39393e-06 + 0.999914 * (_ctx_2048t + 0.3 * jax.random.normal(jax.random.fold_in(_rk, 611), (32, 128, 512), jnp.float32))
        return (x, ctx_2048)
    x, ctx_2048 = _rec_inputs()

    def _L0_xattn_setup():
        import jax, jax.numpy as jnp
        import numpy as np
        EPS = 1e-05

        def _inorm(x):
            m = jnp.mean(x, axis=-1, keepdims=True)
            v = jnp.var(x, axis=-1, keepdims=True)
            return (x - m) * jax.lax.rsqrt(v + EPS)

        def _conv1x1(W, b, x):
            return jnp.einsum('oc,bct->bot', W, x) + b[None, :, None]
        key = jax.random.key(seed)
        ks = jax.random.split(key, 10)
        B, C, T = (4, 128, 512)
        s = 1.0 / np.sqrt(C)
        return {'x_c': jax.random.normal(ks[0], (B, C, T), jnp.float32), 'x_s': jax.random.normal(ks[1], (B, C, T), jnp.float32), 'Wn': jax.random.normal(ks[2], (C, C), jnp.float32) * s, 'bn': jax.random.normal(ks[3], (C,), jnp.float32) * s, 'Wm': jax.random.normal(ks[4], (C, C), jnp.float32) * s, 'bm': jax.random.normal(ks[5], (C,), jnp.float32) * s, 'Wl': jax.random.normal(ks[6], (C, C), jnp.float32) * s, 'bl': jax.random.normal(ks[7], (C,), jnp.float32) * s, 'Wo': jax.random.normal(ks[8], (C, C), jnp.float32) * s, 'bo': jax.random.normal(ks[9], (C,), jnp.float32) * s}
    _L0_xattn_all = _L0_xattn_setup()
    _L0_xattn_in = {k: v for k, v in _L0_xattn_all.items() if k in ('Wn', 'bn', 'Wm', 'bm', 'Wl', 'bl', 'Wo', 'bo')}
    del _L0_xattn_all

    def _L1_xattn_setup():
        import jax, jax.numpy as jnp
        import numpy as np
        E, H, L, B = (512, 32, 256, 4)
        S = E // H
        DM, DD = (32, 64)

        def _ln(x, w, b, eps=1e-05):
            m = x.mean(-1, keepdims=True)
            v = ((x - m) ** 2).mean(-1, keepdims=True)
            return (x - m) / jnp.sqrt(v + eps) * w + b

        def _block(x, state, ln1_w, ln1_b, ln2_w, ln2_b, maa_x, maa_w1, maa_w2, maa_stack, time_decay, td_w1, td_w2, u, Wr, Wk, Wv, Wg, Wo, gn_w, gn_b, ffn_maa_k, ffn_maa_r, Wfk, Wfr, Wfv):
            b, l, e = x.shape
            h = u.shape[0]
            s_ = e // h
            xa = _ln(x, ln1_w, ln1_b)
            sx = jnp.concatenate([state[:, 1:2] - xa[:, :1], xa[:, :-1] - xa[:, 1:]], axis=1)
            xxx = jnp.tanh((xa + sx * maa_x) @ maa_w1).reshape(b, l, 5, DM)
            xxx = jnp.einsum('blfd,fde->blfe', xxx, maa_w2)
            xm = xa[:, :, None] + sx[:, :, None] * (maa_stack + xxx)
            xk, xw, xv, xr, xg = (xm[:, :, j] for j in range(5))
            w = jnp.exp(-jnp.exp(time_decay + jnp.tanh(xw @ td_w1) @ td_w2)).reshape(b, l, h, s_)
            r = (xr @ Wr.T).reshape(b, l, h, s_)
            k = (xk @ Wk.T).reshape(b, l, h, s_)
            v = (xv @ Wv.T).reshape(b, l, h, s_)
            g = jax.nn.silu(xg @ Wg.T)
            s0 = state[:, 2:2 + s_].reshape(b, h, s_, s_)

            def step(s, rkvw):
                r_t, k_t, v_t, w_t = rkvw
                a = k_t[..., :, None] * v_t[..., None, :]
                out = jnp.einsum('bhi,bhij->bhj', r_t, u * a + s)
                s = a + w_t[..., :, None] * s
                return (s, out)
            rkvw = tuple((jnp.moveaxis(t, 1, 0) for t in (r, k, v, w)))
            _, out = jax.lax.scan(step, s0, rkvw)
            out = jnp.moveaxis(out, 0, 1).reshape(b, l, e)
            og = out.reshape(b, l, h, s_)
            m = og.mean(-1, keepdims=True)
            va = ((og - m) ** 2).mean(-1, keepdims=True)
            og = ((og - m) / jnp.sqrt(va + 1e-05)).reshape(b, l, e) * gn_w + gn_b
            x1 = x + og * g @ Wo.T
            xc = _ln(x1, ln2_w, ln2_b)
            sx2 = jnp.concatenate([state[:, 0:1] - xc[:, :1], xc[:, :-1] - xc[:, 1:]], axis=1)
            xk2 = xc + sx2 * ffn_maa_k
            xr2 = xc + sx2 * ffn_maa_r
            rr = jax.nn.sigmoid(xr2 @ Wfr.T)
            kk = jnp.square(jax.nn.relu(xk2 @ Wfk.T))
            return x1 + rr * (kk @ Wfv.T)
        key = jax.random.key(seed)
        ks = jax.random.split(key, 24)
        sc = 0.02
        d = {'x': jax.random.normal(ks[0], (B, L, E), jnp.float32), 'state': jax.random.normal(ks[1], (B, 2 + S, E), jnp.float32) * 0.1, 'ln1_w': jnp.ones((E,), jnp.float32), 'ln1_b': jnp.zeros((E,), jnp.float32), 'ln2_w': jnp.ones((E,), jnp.float32), 'ln2_b': jnp.zeros((E,), jnp.float32), 'maa_x': jax.random.normal(ks[2], (E,), jnp.float32) * 0.1, 'maa_w1': jax.random.normal(ks[3], (E, 5 * DM), jnp.float32) * sc, 'maa_w2': jax.random.normal(ks[4], (5, DM, E), jnp.float32) * sc, 'maa_stack': jax.random.normal(ks[5], (1, 5, E), jnp.float32) * 0.1, 'time_decay': jax.random.normal(ks[6], (E,), jnp.float32) * 0.5, 'td_w1': jax.random.normal(ks[7], (E, DD), jnp.float32) * sc, 'td_w2': jax.random.normal(ks[8], (DD, E), jnp.float32) * sc, 'u': jax.random.normal(ks[9], (H, S, 1), jnp.float32) * 0.1, 'Wr': jax.random.normal(ks[10], (E, E), jnp.float32) * sc, 'Wk': jax.random.normal(ks[11], (E, E), jnp.float32) * sc, 'Wv': jax.random.normal(ks[12], (E, E), jnp.float32) * sc, 'Wg': jax.random.normal(ks[13], (E, E), jnp.float32) * sc, 'Wo': jax.random.normal(ks[14], (E, E), jnp.float32) * sc, 'gn_w': jnp.ones((E,), jnp.float32), 'gn_b': jnp.zeros((E,), jnp.float32), 'ffn_maa_k': jax.random.normal(ks[15], (E,), jnp.float32) * 0.1, 'ffn_maa_r': jax.random.normal(ks[16], (E,), jnp.float32) * 0.1, 'Wfk': jax.random.normal(ks[17], (E, E), jnp.float32) * sc, 'Wfr': jax.random.normal(ks[18], (E, E), jnp.float32) * sc, 'Wfv': jax.random.normal(ks[19], (E, E), jnp.float32) * sc}
        return d
    _L1_xattn_all = _L1_xattn_setup()
    _L1_xattn_in = {k: v for k, v in _L1_xattn_all.items() if k in ('ln1_w', 'ln1_b', 'ln2_w', 'ln2_b', 'maa_x', 'maa_w1', 'maa_w2', 'maa_stack', 'time_decay', 'td_w1', 'td_w2', 'u', 'Wr', 'Wk', 'Wv', 'Wg', 'Wo', 'gn_w', 'gn_b', 'ffn_maa_k', 'ffn_maa_r', 'Wfk', 'Wfr', 'Wfv')}
    del _L1_xattn_all
    return {'x': x, 'ctx_2048': ctx_2048, 'L0_xattn_Wn': _L0_xattn_in['Wn'], 'L0_xattn_bn': _L0_xattn_in['bn'], 'L0_xattn_Wm': _L0_xattn_in['Wm'], 'L0_xattn_bm': _L0_xattn_in['bm'], 'L0_xattn_Wl': _L0_xattn_in['Wl'], 'L0_xattn_bl': _L0_xattn_in['bl'], 'L0_xattn_Wo': _L0_xattn_in['Wo'], 'L0_xattn_bo': _L0_xattn_in['bo'], 'L1_xattn_ln1_w': _L1_xattn_in['ln1_w'], 'L1_xattn_ln1_b': _L1_xattn_in['ln1_b'], 'L1_xattn_ln2_w': _L1_xattn_in['ln2_w'], 'L1_xattn_ln2_b': _L1_xattn_in['ln2_b'], 'L1_xattn_maa_x': _L1_xattn_in['maa_x'], 'L1_xattn_maa_w1': _L1_xattn_in['maa_w1'], 'L1_xattn_maa_w2': _L1_xattn_in['maa_w2'], 'L1_xattn_maa_stack': _L1_xattn_in['maa_stack'], 'L1_xattn_time_decay': _L1_xattn_in['time_decay'], 'L1_xattn_td_w1': _L1_xattn_in['td_w1'], 'L1_xattn_td_w2': _L1_xattn_in['td_w2'], 'L1_xattn_u': _L1_xattn_in['u'], 'L1_xattn_Wr': _L1_xattn_in['Wr'], 'L1_xattn_Wk': _L1_xattn_in['Wk'], 'L1_xattn_Wv': _L1_xattn_in['Wv'], 'L1_xattn_Wg': _L1_xattn_in['Wg'], 'L1_xattn_Wo': _L1_xattn_in['Wo'], 'L1_xattn_gn_w': _L1_xattn_in['gn_w'], 'L1_xattn_gn_b': _L1_xattn_in['gn_b'], 'L1_xattn_ffn_maa_k': _L1_xattn_in['ffn_maa_k'], 'L1_xattn_ffn_maa_r': _L1_xattn_in['ffn_maa_r'], 'L1_xattn_Wfk': _L1_xattn_in['Wfk'], 'L1_xattn_Wfr': _L1_xattn_in['Wfr'], 'L1_xattn_Wfv': _L1_xattn_in['Wfv']}

def reference(x, ctx_2048, L0_xattn_Wn, L0_xattn_bn, L0_xattn_Wm, L0_xattn_bm, L0_xattn_Wl, L0_xattn_bl, L0_xattn_Wo, L0_xattn_bo, L1_xattn_ln1_w, L1_xattn_ln1_b, L1_xattn_ln2_w, L1_xattn_ln2_b, L1_xattn_maa_x, L1_xattn_maa_w1, L1_xattn_maa_w2, L1_xattn_maa_stack, L1_xattn_time_decay, L1_xattn_td_w1, L1_xattn_td_w2, L1_xattn_u, L1_xattn_Wr, L1_xattn_Wk, L1_xattn_Wv, L1_xattn_Wg, L1_xattn_Wo, L1_xattn_gn_w, L1_xattn_gn_b, L1_xattn_ffn_maa_k, L1_xattn_ffn_maa_r, L1_xattn_Wfk, L1_xattn_Wfr, L1_xattn_Wfv):
    import jax
    import jax.numpy as jnp

    def _L0_xattn_ref(x_c, x_s, Wn, bn, Wm, bm, Wl, bl, Wo, bo):
        import jax, jax.numpy as jnp
        import numpy as np
        EPS = 1e-05

        def _inorm(x):
            m = jnp.mean(x, axis=-1, keepdims=True)
            v = jnp.var(x, axis=-1, keepdims=True)
            return (x - m) * jax.lax.rsqrt(v + EPS)

        def _conv1x1(W, b, x):
            return jnp.einsum('oc,bct->bot', W, x) + b[None, :, None]
        Mn = _conv1x1(Wn, bn, _inorm(x_c))
        Mm = _conv1x1(Wm, bm, _inorm(x_s))
        A = jax.nn.softmax(jnp.einsum('bct,bcs->bts', Mn, Mm), axis=-1)
        Ml = _conv1x1(Wl, bl, x_s)
        Mo = jnp.einsum('bcs,bts->bct', Ml, A)
        return _conv1x1(Wo, bo, Mo) + x_c

    def _L1_xattn_ref(x, state, ln1_w, ln1_b, ln2_w, ln2_b, maa_x, maa_w1, maa_w2, maa_stack, time_decay, td_w1, td_w2, u, Wr, Wk, Wv, Wg, Wo, gn_w, gn_b, ffn_maa_k, ffn_maa_r, Wfk, Wfr, Wfv):
        import jax, jax.numpy as jnp
        import numpy as np
        E, H, L, B = (512, 32, 256, 4)
        S = E // H
        DM, DD = (32, 64)

        def _ln(x, w, b, eps=1e-05):
            m = x.mean(-1, keepdims=True)
            v = ((x - m) ** 2).mean(-1, keepdims=True)
            return (x - m) / jnp.sqrt(v + eps) * w + b

        def _block(x, state, ln1_w, ln1_b, ln2_w, ln2_b, maa_x, maa_w1, maa_w2, maa_stack, time_decay, td_w1, td_w2, u, Wr, Wk, Wv, Wg, Wo, gn_w, gn_b, ffn_maa_k, ffn_maa_r, Wfk, Wfr, Wfv):
            b, l, e = x.shape
            h = u.shape[0]
            s_ = e // h
            xa = _ln(x, ln1_w, ln1_b)
            sx = jnp.concatenate([state[:, 1:2] - xa[:, :1], xa[:, :-1] - xa[:, 1:]], axis=1)
            xxx = jnp.tanh((xa + sx * maa_x) @ maa_w1).reshape(b, l, 5, DM)
            xxx = jnp.einsum('blfd,fde->blfe', xxx, maa_w2)
            xm = xa[:, :, None] + sx[:, :, None] * (maa_stack + xxx)
            xk, xw, xv, xr, xg = (xm[:, :, j] for j in range(5))
            w = jnp.exp(-jnp.exp(time_decay + jnp.tanh(xw @ td_w1) @ td_w2)).reshape(b, l, h, s_)
            r = (xr @ Wr.T).reshape(b, l, h, s_)
            k = (xk @ Wk.T).reshape(b, l, h, s_)
            v = (xv @ Wv.T).reshape(b, l, h, s_)
            g = jax.nn.silu(xg @ Wg.T)
            s0 = state[:, 2:2 + s_].reshape(b, h, s_, s_)

            def step(s, rkvw):
                r_t, k_t, v_t, w_t = rkvw
                a = k_t[..., :, None] * v_t[..., None, :]
                out = jnp.einsum('bhi,bhij->bhj', r_t, u * a + s)
                s = a + w_t[..., :, None] * s
                return (s, out)
            rkvw = tuple((jnp.moveaxis(t, 1, 0) for t in (r, k, v, w)))
            _, out = jax.lax.scan(step, s0, rkvw)
            out = jnp.moveaxis(out, 0, 1).reshape(b, l, e)
            og = out.reshape(b, l, h, s_)
            m = og.mean(-1, keepdims=True)
            va = ((og - m) ** 2).mean(-1, keepdims=True)
            og = ((og - m) / jnp.sqrt(va + 1e-05)).reshape(b, l, e) * gn_w + gn_b
            x1 = x + og * g @ Wo.T
            xc = _ln(x1, ln2_w, ln2_b)
            sx2 = jnp.concatenate([state[:, 0:1] - xc[:, :1], xc[:, :-1] - xc[:, 1:]], axis=1)
            xk2 = xc + sx2 * ffn_maa_k
            xr2 = xc + sx2 * ffn_maa_r
            rr = jax.nn.sigmoid(xr2 @ Wfr.T)
            kk = jnp.square(jax.nn.relu(xk2 @ Wfk.T))
            return x1 + rr * (kk @ Wfv.T)
        return _block(x, state, ln1_w, ln1_b, ln2_w, ln2_b, maa_x, maa_w1, maa_w2, maa_stack, time_decay, td_w1, td_w2, u, Wr, Wk, Wv, Wg, Wo, gn_w, gn_b, ffn_maa_k, ffn_maa_r, Wfk, Wfr, Wfv)
    x = _L0_xattn_ref(x, ctx_2048, L0_xattn_Wn, L0_xattn_bn, L0_xattn_Wm, L0_xattn_bm, L0_xattn_Wl, L0_xattn_bl, L0_xattn_Wo, L0_xattn_bo)
    x = _L1_xattn_ref(x, ctx_2048, L1_xattn_ln1_w, L1_xattn_ln1_b, L1_xattn_ln2_w, L1_xattn_ln2_b, L1_xattn_maa_x, L1_xattn_maa_w1, L1_xattn_maa_w2, L1_xattn_maa_stack, L1_xattn_time_decay, L1_xattn_td_w1, L1_xattn_td_w2, L1_xattn_u, L1_xattn_Wr, L1_xattn_Wk, L1_xattn_Wv, L1_xattn_Wg, L1_xattn_Wo, L1_xattn_gn_w, L1_xattn_gn_b, L1_xattn_ffn_maa_k, L1_xattn_ffn_maa_r, L1_xattn_Wfk, L1_xattn_Wfr, L1_xattn_Wfv)
    return x

_drawn_inputs = setup_inputs


def setup_inputs(seed=0):
    import zlib

    import numpy as np

    out = dict(_drawn_inputs(seed))
    spreads = {'L1_xattn_ln1_w': (1.0, 0.2),
     'L1_xattn_ln1_b': (0.0, 0.448),
     'L1_xattn_ln2_w': (1.0, 0.6),
     'L1_xattn_ln2_b': (0.0, 0.8),
     'L1_xattn_gn_w': (1.0, 0.6),
     'L1_xattn_gn_b': (0.0, 0.8)}
    factors = {'L0_xattn_bm': 8.0,
     'L1_xattn_maa_x': 8.0,
     'L1_xattn_maa_w1': 4.756,
     'L1_xattn_maa_w2': 4.708,
     'L1_xattn_td_w1': 8.0,
     'L1_xattn_td_w2': 8.0,
     'L1_xattn_u': 5.056,
     'L1_xattn_ffn_maa_k': 8.0,
     'L1_xattn_ffn_maa_r': 8.0,
     'L1_xattn_Wfr': 6.67}
    for name, (base, spread) in spreads.items():
        noise = np.random.default_rng([zlib.crc32(name.encode()), seed]).standard_normal(out[name].shape)
        drawn = base * np.exp(spread * noise) if base else spread * noise
        out[name] = jnp.asarray(drawn.astype(out[name].dtype))
    for name, factor in factors.items():
        out[name] = (out[name] * factor).astype(out[name].dtype)
    return out
```

```python
from contextlib import ExitStack

import concourse.bass as bass
from concourse import mybir

F32 = mybir.dt.float32
ALU = mybir.AluOpType
ACT = mybir.ActivationFunctionType
X = mybir.AxisListType.X

NB = 32
P = 128
E = 512
C = E // P
HS = 16
H = E // HS
HC = H // C
DM = 32
DD = 64
EPS = 1e-5
MIX = "kwvrg"
ORDER = "vwkrg"

COLS = {"ln1_w": 0, "ln1_b": 4, "ln2_w": 8, "ln2_b": 12, "maa_x": 16, "time_decay": 20,
        "ffn_maa_k": 24, "ffn_maa_r": 28, "u": 32, "maa_stack": 36, "bn": 56, "bm": 57, "bl": 58, "bo": 59}
NPAR = 60
BIG = ["Wv", "Wk", "Wr", "Wg", "Wo", "Wfk", "Wfr", "Wfv"]
ST0, ST1, STS, NST = 0, C, 2 * C, 2 * C + C * HS


class Steps:

    def __init__(self, sem, labels):
        self.sem, self.at = sem, {x: k for k, x in enumerate(labels.split())}

    def count(self, label, n):
        if isinstance(n, int) and n < 0:
            return 0
        return n * len(self.at) + self.at[label] + 1



def late(m):
    return not (isinstance(m, int) and m == 0)


def held(eng, register, value):
    if isinstance(value, int):
        return value
    eng.reg_mov(register, value)
    return register


FRONT_JOBS = "Mn Mm V S0 S1 S2 S3 T0 T1 T2 T3 O Tx W1 Mv Mw Vp TvN D1 Mk D2 Kp Mr Rp Mg G".split()
BACK_JOBS = "C To Wo Tx2 FK FR FV".split()
FRONT_BANKS, BACK_BANKS, WKV_BANK = [0, 1, 2, 3, 5], [6, 7], 4


def build(nc, x_c, x_s, state, params, att_w, big_w, maa_w1, maa_w2, td_w1, td_w2, gn, out, v_dram):
    with ExitStack() as ctx:
        def sb(name, shape):
            return ctx.enter_context(nc.sbuf_tensor(name, shape, F32))

        def sem(name):
            return ctx.enter_context(nc.semaphore(name))

        bank = [ctx.enter_context(nc.psum_tensor(f"bank{i}", [P, E], F32)) for i in range(8)]

        ident = sb("ident", [P, P])
        head_sum = sb("head_sum", [P, HC])
        mhalf = sb("mhalf", [P, H])
        par = sb("par", [P, NPAR])
        attw = sb("attw", [P, 4, P])
        wolT = sb("wolT", [P, P])
        bl_rep = sb("bl_rep", [P, P])
        vbias = sb("vbias", [P, P])
        W = {name: sb(name, [P, C, E]) for name in BIG}
        w1 = sb("w1", [P, C, 5 * DM])
        w2 = sb("w2", [P, E])
        w2g = sb("w2g", [DM, E])
        tw1 = sb("tw1", [P, C, DD])
        tw2 = sb("tw2", [DD, E])
        gnw = sb("gnw", [P, 2, E])

        xc = sb("xc", [P, 2, E])
        xs = sb("xs", [P, 2, E])
        st = sb("st", [P, 2, NST])
        st6 = sb("st6", [P, 3, 6])
        mv = sb("mv", [P, 3, 2])
        ve = sb("ve", [P, 4])
        rstd = sb("rstd", [P, 4])
        xn = sb("xn", [P, E])
        yn = sb("yn", [P, E])
        Mn = sb("Mn", [P, E])
        Mm = sb("Mm", [P, E])
        vT_att = sb("vT_att", [P, C, P])
        prob = sb("prob", [P, C, E])
        probT = sb("probT", [P, C, E])
        nmax = sb("nmax", [P, C])
        rsum = sb("rsum", [P, C])
        rinv = sb("rinv", [P, C])
        xa = sb("xa", [P, C, P + 1])
        tx = sb("tx", [P, P])
        txg = sb("txg", [DM, P])
        xf = sb("xf", [P, 2, C, P])
        dt = sb("dt", [DD, P])
        vT = sb("vT", [P, C, P])
        xin = sb("xin", [P, 2, E])
        kT = sb("kT", [P, 2, C, P])
        rT = sb("rT", [P, 2, C, P])
        wT = sb("wT", [P, 2, C, P])
        vN = sb("vN", [P, 2, E])
        gN = sb("gN", [P, 2, E])
        hst = sb("hst", [P, 2, NST])
        rku = sb("rku", [P, C, P])
        vrep = sb("vrep", [P, 2, HS, P])
        S = sb("S", [P, 2, HS, P])
        og = sb("og", [P, E])
        sq = sb("sq", [P, E])
        gw = sb("gw", [P, E])
        gb = sb("gb", [P, E])
        hsum = sb("hsum", [P, 2, H])
        hve = sb("hve", [P, H])
        hrs = sb("hrs", [P, H])
        x1 = sb("x1", [P, E])
        st62 = sb("st62", [P, 6])
        mv2 = sb("mv2", [P, 2])
        ve2 = sb("ve2", [P, 1])
        rstd2 = sb("rstd2", [P, 1])
        xc2 = sb("xc2", [P, C, P + 1])
        kr = sb("kr", [P, C, P])
        rr = sb("rr", [P, E])

        def by_chunk(ap):
            return ap.rearrange("p (c t) -> p c t", c=C)

        sx = by_chunk(probT[:, 0, :])
        xx = by_chunk(probT[:, 1, :])
        mt = probT[:, 2:4, :].rearrange("p b (c t) -> p b c t", c=C)
        xhat = Mm
        th = Mn
        ez = by_chunk(yn[:, :])
        ogT = by_chunk(xn[:, :])
        xhat2 = sq
        sx2 = rku
        xk2 = by_chunk(gw[:, :])
        xr2 = by_chunk(gb[:, :])
        kk = kr
        y = rr
        ob = og

        def col(name, c, f=0):
            k = COLS[name] + C * f + c
            return par[:, k:k + 1]

        setup_loaded = [sem(f"setup_loaded{i}") for i in range(4)]
        x_loaded = [sem(f"x_loaded{i}") for i in range(2)]
        vrep_loaded = [sem(f"vrep_loaded{i}") for i in range(2)]
        v_stored = sem("v_stored")
        out_stored = sem("out_stored")
        pool_const = sem("pool_const")
        pe_setup = sem("pe_setup")
        act_setup = sem("act_setup")
        dve_setup = sem("dve_setup")
        dve_front = Steps(sem("vector_front"), "stats aggr xn yn vatt mx0 mx1 ri0 pn0 mx2 ri1 pn1 mx3 ri2 pn2 ri3 pn3 "
                                        "xin xst xag xhat sx xx mv mw mk mr mg g")
        dve_back = Steps(sem("vector_back"), "a0 s0 q0 a1 s1 q1 a2 s2 q2 a3 s3 q3 "
                                       "o1 o2 sum oc var o3 o4 o5 x1 st ag xh sx2 xk2 xr2 rr y")
        act_front = Steps(sem("scalar_front"), "Mn Mm p0 p1 p2 p3 T0 T1 T2 T3 xa tx vT vN dt ez1 w k r th")
        act_back = Steps(sem("scalar_back"), "oT xc2 kr thr")
        pool_front = Steps(sem("gpsimd_front"), "ve rstd hst xa0 ve1 rstd1 fv fw fk fr fg")
        pool_back = Steps(sem("gpsimd_back"), "rk rku s0 s1 s2 s3 gw gb sq hve hrs ve2 rstd2 xc20 kk out")
        pe_front = Steps(sem("tensor_front"), " ".join(FRONT_JOBS))
        pe_back = Steps(sem("tensor_back"), "C red0 red1 red2 red3 To Wo Tx2 FK FR FV")

        front_reader = {"Mn": (act_front, "Mn"), "Mm": (act_front, "Mm"), "V": (dve_front, "vatt"), "O": (dve_front, "xin"), "Tx": (act_front, "xa"),
                        "W1": (act_front, "tx"), "Vp": (act_front, "vT"), "TvN": (act_front, "vN"), "D1": (act_front, "dt"), "D2": (act_front, "ez1"),
                        "Kp": (act_front, "k"), "Rp": (act_front, "r"), "G": (dve_front, "g")}
        front_reader.update({f"S{i}": (act_front, f"p{i}") for i in range(C)})
        front_reader.update({f"T{i}": (act_front, f"T{i}") for i in range(C)})
        front_reader.update({f"M{f}": (dve_front, f"m{f}") for f in MIX})
        back_reader = {"C": (dve_back, "o1"), "To": (act_back, "oT"), "Wo": (dve_back, "x1"), "Tx2": (act_back, "xc2"), "FK": (act_back, "kr"),
                       "FR": (act_back, "thr"), "FV": (dve_back, "y")}

        def bank_of(job):
            if job in FRONT_JOBS:
                return bank[FRONT_BANKS[FRONT_JOBS.index(job) % len(FRONT_BANKS)]]
            return bank[BACK_BANKS[BACK_JOBS.index(job) % len(BACK_BANKS)]]

        def bank_free(job, n):
            jobs, banks, reader = ((FRONT_JOBS, FRONT_BANKS, front_reader) if job in FRONT_JOBS
                                   else (BACK_JOBS, BACK_BANKS, back_reader))
            q = jobs.index(job) - len(banks)
            lag = 0
            if q < 0:
                q += len(banks)
                while q + len(banks) < len(jobs):
                    q += len(banks)
                lag = 1
            steps, label = reader[jobs[q]]
            return steps.sem, steps.count(label, n - lag)

        block = ctx.enter_context(nc.Block())

        def run(eng, step, front, back):
            front(0, 0, 0)
            step(1, 0, 1)
            with eng.Fori(0, (NB - 2) // 2) as i:
                step(i * 2 + 2, i + 1, 0)
                step(i * 2 + 3, i + 1, 1)
            back(NB - 1, 1 - NB % 2)

        @block.sync
        def _(sp):
            regs = [sp.alloc_register(f"sync_wait{i}") for i in range(2)]
            sp.dma_start(attw[:, :, :], att_w).then_inc(setup_loaded[0], 16)
            sp.dma_start(par[:, :], params).then_inc(setup_loaded[0], 16)

            def load_x(n, m, p):
                if late(m):
                    v0 = held(sp, regs[0], dve_front.count("xin", n - 2))
                    v1 = held(sp, regs[1], pool_front.count("xa0", n - 2))
                    sp.wait_ge(setup_loaded[0], 32)
                    sp.wait_ge(dve_front.sem, v0)
                    sp.wait_ge(pool_front.sem, v1)
                if isinstance(n, int):
                    src = (x_c[n], x_s[n], state[n])
                else:
                    src = tuple(a[bass.ds(n, 1)].rearrange("o p f -> (o p) f") for a in (x_c, x_s, state))
                sp.dma_start(xc[:, p, :], src[0]).then_inc(x_loaded[p], 16)
                sp.dma_start(xs[:, p, :], src[1]).then_inc(x_loaded[p], 16)
                sp.dma_start(st[:, p, :], src[2]).then_inc(x_loaded[p], 16)

            def load_vrep(b, q):
                src = v_dram[q].rearrange("(c h j) t -> c h (j t)", c=C, h=HC)
                for c in range(C):
                    v0 = held(sp, regs[0], 16 * (b + 1))
                    v1 = held(sp, regs[1], dve_back.count(f"s{(c + 2) % C}", b if c >= 2 else b - 1))
                    sp.wait_ge(setup_loaded[0], 32)
                    sp.wait_ge(v_stored, v0)
                    sp.wait_ge(dve_back.sem, v1)
                    sp.dma_start(vrep[:, c % 2, :, :].rearrange("p j t -> p (j t)"),
                                 src[c].unsqueeze(1).broadcast_to([HC, HS, HS * P])).then_inc(vrep_loaded[c % 2], 16)

            load_x(0, 0, 0)
            load_x(1, 0, 1)
            sp.dma_start(w1[:, :, :], maa_w1).then_inc(setup_loaded[1], 16)
            sp.dma_start(w2[:, :], maa_w2[0:P, :]).then_inc(setup_loaded[1], 16)
            sp.dma_start(w2g[:, :], maa_w2[P:P + DM, :]).then_inc(setup_loaded[1], 16)
            sp.dma_start(tw1[:, :, :], td_w1).then_inc(setup_loaded[1], 16)
            sp.dma_start(tw2[:, :], td_w2).then_inc(setup_loaded[1], 16)
            for k, name in enumerate(BIG):
                sp.dma_start(W[name][:, :, :], big_w[k]).then_inc(setup_loaded[2], 16)
            sp.dma_start(gnw[:, :, :], gn.unsqueeze(0).broadcast_to([P, 2, E])).then_inc(setup_loaded[3], 16)

            def step(n, m, p):
                if late(n - 1):
                    load_x(n, m, p)
                load_vrep(n - 1, 1 - p)

            run(sp, step, lambda n, m, p: None, load_vrep)

        @block.gpsimd
        def _(eng):
            po = nc.gpsimd
            regs = [eng.alloc_register(f"pool_wait{i}") for i in range(3)]
            po.memset(ident[:, :], 0.0).then_inc(pool_const, 1)
            po.memset(head_sum[:, :], 1.0).then_inc(pool_const, 1)
            po.memset(mhalf[:, :], -0.5).then_inc(pool_const, 1)
            eng.wait_ge(pool_const, 3)
            po.affine_select(out=ident[:, :], in_=ident[:, :], compare_op=ALU.not_equal, fill=1.0, base=0,
                             pattern=[[-1, P]], channel_multiplier=1).then_inc(pool_const, 1)
            po.affine_select(out=head_sum[:, :], in_=head_sum[:, :], compare_op=ALU.is_ge, fill=0.0, base=0,
                             pattern=[[-HS, HC]], channel_multiplier=1).then_inc(pool_const, 1)
            eng.wait_ge(pool_const, 5)
            po.affine_select(out=head_sum[:, :], in_=head_sum[:, :], compare_op=ALU.is_ge, fill=0.0, base=HS - 1,
                             pattern=[[HS, HC]], channel_multiplier=-1).then_inc(pool_const, 1)
            eng.wait_ge(setup_loaded[3], 16)
            po.tensor_scalar(gnw[:, :, :], gnw[:, :, :], 0.5, None, ALU.mult).then_inc(pool_const, 1)
            eng.wait_ge(pool_const, 7)

            def rstd_of(res, var, tmp, scale, var_sem, var_count, own, own_label, n):
                v0 = held(eng, regs[0], var_count)
                eng.wait_ge(pool_const, 7)
                eng.wait_ge(var_sem, v0)
                po.tensor_scalar(tmp, var, scale, EPS, ALU.mult, ALU.add).then_inc(own.sem, 1)
                eng.wait_ge(own.sem, own.count(own_label, n))
                po.tensor_tensor(res, tmp, mhalf[:, 0:tmp.shape[1]], ALU.pow).then_inc(own.sem, 1)

            def f_norm(n, m, p):
                rstd_of(rstd[:, 0:2], mv[:, 0:2, 1], ve[:, 0:2], 1.0, dve_front.sem, dve_front.count("aggr", n), pool_front, "ve", n)
                v0 = held(eng, regs[0], 48 * (m + 1))
                if late(m):
                    v1 = held(eng, regs[1], pool_back.count("xc20", n - 2))
                    v2 = held(eng, regs[2], dve_back.count("s3", n - 2))
                eng.wait_ge(pool_const, 7)
                eng.wait_ge(x_loaded[p], v0)
                if late(m):
                    eng.wait_ge(pool_back.sem, v1)
                    eng.wait_ge(dve_back.sem, v2)
                po.tensor_copy(hst[:, p, :], st[:, p, :]).then_inc(pool_front.sem, 1)
                v0 = held(eng, regs[0], dve_front.count("xx", n - 1))
                v1 = held(eng, regs[1], pool_front.count("fg", n - 1))
                eng.wait_ge(pool_const, 7)
                eng.wait_ge(dve_front.sem, v0)
                eng.wait_ge(pool_front.sem, v1)
                po.tensor_copy(xa[:, :, 0], st[:, p, ST1:ST1 + C]).then_inc(pool_front.sem, 1)

            def f_norm1(n, m, p):
                rstd_of(rstd[:, 2:3], mv[:, 2:3, 1], ve[:, 2:3], 1.0, dve_front.sem, dve_front.count("xag", n), pool_front, "ve1", n)

            def f_mix(n, i):
                f, b = ORDER[i], i % 2
                eng.wait_ge(dve_front.sem, dve_front.count(f"m{f}", n))
                eng.wait_ge(act_front.sem, act_front.count("xa", n))
                user = {"v": "G", "w": "Rp", "k": "Vp", "r": "D1", "g": "Kp"}[f]
                eng.wait_ge(pe_front.sem, pe_front.count(user, n - 1 if i < 2 else n))
                po.tensor_tensor(xf[:, b, :, :], mt[:, b, :, :], xa[:, :, 1:P + 1], ALU.add).then_inc(pool_front.sem, 1)

            def b_rku(b, q):
                eng.wait_ge(act_front.sem, act_front.count("k", b))
                eng.wait_ge(act_front.sem, act_front.count("r", b))
                eng.wait_ge(dve_back.sem, dve_back.count("xr2", b - 1))
                po.tensor_tensor(rku[:, :, :], rT[:, q, :, :], kT[:, q, :, :], ALU.mult).then_inc(pool_back.sem, 1)
                eng.wait_ge(pool_back.sem, pool_back.count("rk", b))
                u_b = par[:, COLS["u"]:COLS["u"] + C].unsqueeze(2).broadcast_to([P, C, P])
                po.tensor_tensor(rku[:, :, :], rku[:, :, :], u_b, ALU.mult).then_inc(pool_back.sem, 1)

            def b_s0(b, q, c):
                v0 = held(eng, regs[0], pool_front.count("hst", b))
                v1 = held(eng, regs[1], pe_back.count(f"red{(c + 2) % C}", b if c >= 2 else b - 1))
                eng.wait_ge(pool_const, 7)
                eng.wait_ge(pool_front.sem, v0)
                eng.wait_ge(pe_back.sem, v1)
                po.tensor_copy(S[:, c % 2, :, 0], hst[:, q, STS + HS * c:STS + HS * c + HS]).then_inc(pool_back.sem, 1)

            def b_gate(b, q):
                eng.wait_ge(dve_front.sem, dve_front.count("g", b))
                eng.wait_ge(pe_back.sem, pe_back.count("FR", b - 1))
                po.tensor_tensor(gw[:, :], gN[:, q, :], gnw[:, 0, :], ALU.mult).then_inc(pool_back.sem, 1)
                po.tensor_tensor(gb[:, :], gN[:, q, :], gnw[:, 1, :], ALU.mult).then_inc(pool_back.sem, 1)

            def b_sq(b):
                eng.wait_ge(dve_back.sem, dve_back.count("oc", b))
                po.tensor_tensor(sq[:, :], og[:, :], og[:, :], ALU.mult).then_inc(pool_back.sem, 1)

            def b_hrs(b):
                rstd_of(hrs[:, :], hsum[:, 1, :], hve[:, :], 1.0 / HS, dve_back.sem, dve_back.count("var", b), pool_back, "hve", b)

            def b_norm2(b):
                rstd_of(rstd2[:, :], mv2[:, 1:2], ve2[:, :], 1.0, dve_back.sem, dve_back.count("ag", b), pool_back, "ve2", b)

            def b_xc20(b, q):
                v0 = held(eng, regs[0], dve_back.count("xr2", b - 1))
                eng.wait_ge(pool_const, 7)
                eng.wait_ge(dve_back.sem, v0)
                po.tensor_copy(xc2[:, :, 0], hst[:, q, ST0:ST0 + C]).then_inc(pool_back.sem, 1)

            def b_kk(b):
                eng.wait_ge(act_back.sem, act_back.count("kr", b))
                eng.wait_ge(pe_back.sem, pe_back.count("FV", b - 1))
                po.tensor_tensor(kk[:, :, :], kr[:, :, :], kr[:, :, :], ALU.mult).then_inc(pool_back.sem, 1)

            def b_out(b):
                eng.wait_ge(dve_back.sem, dve_back.count("y", b))
                po.tensor_tensor(ob[:, :], y[:, :], x1[:, :], ALU.add).then_inc(pool_back.sem, 1)

            def front(n, m, p):
                f_norm(n, m, p)
                f_norm1(n, m, p)
                for i in range(5):
                    f_mix(n, i)

            def back(b, q):
                b_rku(b, q)
                for c in range(C):
                    b_s0(b, q, c)
                b_gate(b, q)
                b_sq(b)
                b_hrs(b)
                b_norm2(b)
                b_xc20(b, q)
                b_kk(b)
                b_out(b)

            def step(n, m, p):
                b, q = n - 1, 1 - p
                b_rku(b, q)
                b_s0(b, q, 0)
                b_s0(b, q, 1)
                f_norm(n, m, p)
                b_s0(b, q, 2)
                f_norm1(n, m, p)
                b_s0(b, q, 3)
                b_gate(b, q)
                f_mix(n, 0)
                b_sq(b)
                f_mix(n, 1)
                b_hrs(b)
                f_mix(n, 2)
                f_mix(n, 3)
                b_norm2(b)
                b_xc20(b, q)
                f_mix(n, 4)
                b_kk(b)
                b_out(b)

            run(eng, step, front, back)

        @block.vector
        def _(eng):
            ve_ = nc.vector
            regs = [eng.alloc_register("vector_wait")]
            eng.wait_ge(setup_loaded[0], 32)
            ve_.tensor_copy(bl_rep[:, :], par[:, COLS["bl"]:COLS["bl"] + 1].broadcast_to([P, P])).then_inc(dve_setup, 1)
            eng.wait_ge(pe_setup, 2)
            ve_.tensor_copy(wolT[:, :], bank[0][:, 0:P]).then_inc(dve_setup, 1)
            ve_.tensor_copy(vbias[:, :], bank[1][:, 0:P]).then_inc(dve_setup, 1)
            eng.wait_ge(dve_setup, 3)

            def f_stats(n, m, p):
                eng.wait_ge(x_loaded[p], 48 * (m + 1))
                ve_.bn_stats(st6[:, 0, :], xc[:, p, :])
                ve_.bn_stats(st6[:, 1, :], xs[:, p, :]).then_inc(dve_front.sem, 1)
                v0 = held(eng, regs[0], dve_front.count("stats", n))
                eng.wait_ge(dve_setup, 3)
                eng.wait_ge(dve_front.sem, v0)
                ve_.bn_aggr(mv[:, 0, :], st6[:, 0, :])
                ve_.bn_aggr(mv[:, 1, :], st6[:, 1, :]).then_inc(dve_front.sem, 1)

            def f_norm(n, m, p):
                eng.wait_ge(pool_front.sem, pool_front.count("rstd", n))
                eng.wait_ge(dve_front.sem, dve_front.count("aggr", n))
                eng.wait_ge(pe_back.sem, pe_back.count("Wo", n - 2))
                ve_.tensor_scalar(xn[:, :], xc[:, p, :], mv[:, 0, 0:1], rstd[:, 0:1],
                                  ALU.subtract, ALU.mult).then_inc(dve_front.sem, 1)
                ve_.tensor_scalar(yn[:, :], xs[:, p, :], mv[:, 1, 0:1], rstd[:, 1:2],
                                  ALU.subtract, ALU.mult).then_inc(dve_front.sem, 1)

            def f_vatt(n):
                eng.wait_ge(pe_front.sem, pe_front.count("V", n))
                ve_.tensor_tensor(vT_att[:, :, :], bank_of("V")[:, :].rearrange("p (s o) -> p s o", s=C),
                                  vbias[:, :].unsqueeze(1).broadcast_to([P, C, P]), ALU.add).then_inc(dve_front.sem, 1)

            def f_max(n, t):
                eng.wait_ge(pe_front.sem, pe_front.count(f"S{t}", n))
                ve_.tensor_reduce(nmax[:, t:t + 1], bank_of(f"S{t}")[:, :], X, ALU.max, negate=True).then_inc(dve_front.sem, 1)

            def f_probs(n, t):
                eng.wait_ge(act_front.sem, act_front.count(f"p{t}", n))
                ve_.reciprocal(rinv[:, t:t + 1], rsum[:, t:t + 1]).then_inc(dve_front.sem, 1)
                eng.wait_ge(dve_front.sem, dve_front.count(f"ri{t}", n))
                ve_.tensor_scalar(prob[:, t, :], prob[:, t, :], rinv[:, t:t + 1], None, ALU.mult).then_inc(dve_front.sem, 1)

            def f_xin(n, m, p):
                eng.wait_ge(pe_front.sem, pe_front.count("O", n))
                ve_.scalar_tensor_tensor(xin[:, p, :], bank_of("O")[:, :], col("bo", 0), xc[:, p, :],
                                         ALU.add, ALU.add).then_inc(dve_front.sem, 1)
                eng.wait_ge(dve_front.sem, dve_front.count("xin", n))
                ve_.bn_stats(st6[:, 2, :], xin[:, p, :]).then_inc(dve_front.sem, 1)
                v0 = held(eng, regs[0], dve_front.count("xst", n))
                eng.wait_ge(dve_setup, 3)
                eng.wait_ge(dve_front.sem, v0)
                ve_.bn_aggr(mv[:, 2, :], st6[:, 2, :]).then_inc(dve_front.sem, 1)

            def f_xhat(n, m, p):
                eng.wait_ge(pool_front.sem, pool_front.count("rstd1", n))
                ve_.tensor_scalar(xhat[:, :], xin[:, p, :], mv[:, 2, 0:1], rstd[:, 2:3],
                                  ALU.subtract, ALU.mult).then_inc(dve_front.sem, 1)

            def f_shift(n):
                eng.wait_ge(act_front.sem, act_front.count("xa", n))
                eng.wait_ge(pool_front.sem, pool_front.count("xa0", n))
                ve_.tensor_tensor(sx[:, :, :], xa[:, :, 0:P], xa[:, :, 1:P + 1], ALU.subtract).then_inc(dve_front.sem, 1)
                eng.wait_ge(dve_front.sem, dve_front.count("sx", n))
                for c in range(C):
                    last = ve_.scalar_tensor_tensor(xx[:, c, :], sx[:, c, :], col("maa_x", c), xa[:, c, 1:P + 1],
                                                    ALU.mult, ALU.add)
                last.then_inc(dve_front.sem, 1)

            def f_mix(n, i):
                f, b = ORDER[i], i % 2
                eng.wait_ge(pe_front.sem, pe_front.count(f"M{f}", n))
                if i >= 2:
                    eng.wait_ge(pool_front.sem, pool_front.count(f"f{ORDER[i - 2]}", n))
                ps = bank_of(f"M{f}")
                for c in range(C):
                    last = ve_.scalar_tensor_tensor(mt[:, b, c, :], ps[:, c * P:(c + 1) * P],
                                                    col("maa_stack", c, MIX.index(f)), sx[:, c, :], ALU.add, ALU.mult)
                last.then_inc(dve_front.sem, 1)

            def f_gate(n, m, p):
                eng.wait_ge(act_front.sem, act_front.count("th", n))
                if late(m):
                    eng.wait_ge(pool_back.sem, pool_back.count("gb", n - 2))
                ve_.scalar_tensor_tensor(gN[:, p, :], th[:, :], 1.0, bank_of("G")[:, :],
                                         ALU.add, ALU.mult).then_inc(dve_front.sem, 1)

            def b_outer(b, q, c):
                eng.wait_ge(vrep_loaded[c % 2], 16 * (b * (C // 2) + c // 2 + 1))
                if c == 0:
                    eng.wait_ge(act_front.sem, act_front.count("k", b))
                v = vrep[:, c % 2, :, :]
                ve_.tensor_tensor(v, v, kT[:, q, c, :].unsqueeze(1).broadcast_to([P, HS, P]),
                                  ALU.mult).then_inc(dve_back.sem, 1)

            def b_scan(b, q, c, j0, j1):
                if j0 == 0:
                    eng.wait_ge(dve_back.sem, dve_back.count(f"a{c}", b))
                    eng.wait_ge(act_front.sem, act_front.count("w", b))
                    eng.wait_ge(pool_front.sem, pool_front.count("hst", b))
                    eng.wait_ge(pool_back.sem, pool_back.count(f"s{c}", b))
                for j in range(j0, j1):
                    k = STS + HS * c + j
                    last = ve_.tensor_tensor_scan(S[:, c % 2, j, 1:P], wT[:, q, c, 0:P - 1], vrep[:, c % 2, j, 0:P - 1],
                                                  hst[:, q, k:k + 1], ALU.mult, ALU.add)
                if j1 == HS:
                    last.then_inc(dve_back.sem, 1)

            def b_read(b, q, c):
                eng.wait_ge(dve_back.sem, dve_back.count(f"s{c}", b))
                if c == 0:
                    eng.wait_ge(act_front.sem, act_front.count("r", b))
                s = S[:, c % 2, :, :]
                ve_.tensor_tensor(s, s, rT[:, q, c, :].unsqueeze(1).broadcast_to([P, HS, P]),
                                  ALU.mult).then_inc(dve_back.sem, 1)

            def heads(ap):
                return ap.rearrange("p (h j) -> p h j", j=HS)

            def over_head(ap):
                return ap.unsqueeze(2).broadcast_to([P, H, HS])

            def b_og(b, q):
                eng.wait_ge(pe_back.sem, pe_back.count("C", b))
                eng.wait_ge(act_front.sem, act_front.count("vN", b))
                if late(b):
                    eng.wait_ge(out_stored, 16 * b)
                ve_.tensor_tensor(heads(og[:, :]), heads(vN[:, q, :]), over_head(bank_of("C")[:, 0:H]),
                                  ALU.mult).then_inc(dve_back.sem, 1)
                eng.wait_ge(dve_back.sem, dve_back.count("o1", b))
                eng.wait_ge(pe_back.sem, pe_back.count("red3", b))
                ve_.tensor_tensor(og[:, :], og[:, :], bank[WKV_BANK][:, :], ALU.add).then_inc(dve_back.sem, 1)
                eng.wait_ge(dve_back.sem, dve_back.count("o2", b))
                ve_.tensor_reduce(hsum[:, 0, :], heads(og[:, :]), X, ALU.add).then_inc(dve_back.sem, 1)
                eng.wait_ge(dve_back.sem, dve_back.count("sum", b))
                ve_.scalar_tensor_tensor(heads(og[:, :]), over_head(hsum[:, 0, :]), -1.0 / HS, heads(og[:, :]),
                                         ALU.mult, ALU.add).then_inc(dve_back.sem, 1)

            def b_var(b):
                eng.wait_ge(pool_back.sem, pool_back.count("sq", b))
                ve_.tensor_reduce(hsum[:, 1, :], heads(sq[:, :]), X, ALU.add).then_inc(dve_back.sem, 1)

            def b_gn(b):
                eng.wait_ge(pool_back.sem, pool_back.count("hrs", b))
                eng.wait_ge(dve_back.sem, dve_back.count("oc", b))
                ve_.tensor_tensor(heads(og[:, :]), heads(og[:, :]), over_head(hrs[:, :]), ALU.mult).then_inc(dve_back.sem, 1)
                eng.wait_ge(dve_back.sem, dve_back.count("o3", b))
                eng.wait_ge(pool_back.sem, pool_back.count("gb", b))
                ve_.tensor_tensor(og[:, :], og[:, :], gw[:, :], ALU.mult).then_inc(dve_back.sem, 1)
                eng.wait_ge(dve_back.sem, dve_back.count("o4", b))
                ve_.tensor_tensor(og[:, :], og[:, :], gb[:, :], ALU.add).then_inc(dve_back.sem, 1)

            def b_x1(b, q):
                eng.wait_ge(pe_back.sem, pe_back.count("Wo", b))
                eng.wait_ge(pool_back.sem, pool_back.count("out", b - 1))
                ve_.tensor_tensor(x1[:, :], bank_of("Wo")[:, :], xin[:, q, :], ALU.add).then_inc(dve_back.sem, 1)
                eng.wait_ge(dve_back.sem, dve_back.count("x1", b))
                ve_.bn_stats(st62[:, :], x1[:, :]).then_inc(dve_back.sem, 1)
                v0 = held(eng, regs[0], dve_back.count("st", b))
                eng.wait_ge(dve_setup, 3)
                eng.wait_ge(dve_back.sem, v0)
                ve_.bn_aggr(mv2[:, :], st62[:, :]).then_inc(dve_back.sem, 1)

            def b_xhat(b):
                eng.wait_ge(pool_back.sem, pool_back.count("rstd2", b))
                ve_.tensor_scalar(xhat2[:, :], x1[:, :], mv2[:, 0:1], rstd2[:, 0:1],
                                  ALU.subtract, ALU.mult).then_inc(dve_back.sem, 1)

            def b_shift(b):
                eng.wait_ge(act_back.sem, act_back.count("xc2", b))
                eng.wait_ge(pool_back.sem, pool_back.count("xc20", b))
                ve_.tensor_tensor(sx2[:, :, :], xc2[:, :, 0:P], xc2[:, :, 1:P + 1], ALU.subtract).then_inc(dve_back.sem, 1)
                eng.wait_ge(dve_back.sem, dve_back.count("sx2", b))
                for dst, mix in ((xk2, "ffn_maa_k"), (xr2, "ffn_maa_r")):
                    for c in range(C):
                        last = ve_.scalar_tensor_tensor(dst[:, c, :], sx2[:, c, :], col(mix, c), xc2[:, c, 1:P + 1],
                                                        ALU.mult, ALU.add)
                    last.then_inc(dve_back.sem, 1)

            def b_y(b):
                eng.wait_ge(act_back.sem, act_back.count("thr", b))
                ve_.tensor_scalar(rr[:, :], rr[:, :], 0.5, 0.5, ALU.mult, ALU.add).then_inc(dve_back.sem, 1)
                eng.wait_ge(dve_back.sem, dve_back.count("rr", b))
                eng.wait_ge(pe_back.sem, pe_back.count("FV", b))
                ve_.tensor_tensor(y[:, :], bank_of("FV")[:, :], rr[:, :], ALU.mult).then_inc(dve_back.sem, 1)

            def front(n, m, p):
                f_stats(n, m, p)
                f_norm(n, m, p)
                f_vatt(n)
                f_max(n, 0)
                f_max(n, 1)
                f_probs(n, 0)
                f_max(n, 2)
                f_probs(n, 1)
                f_max(n, 3)
                f_probs(n, 2)
                f_probs(n, 3)
                f_xin(n, m, p)
                f_xhat(n, m, p)
                f_shift(n)
                for i in range(5):
                    f_mix(n, i)
                f_gate(n, m, p)

            def back(b, q):
                for c in range(C):
                    b_outer(b, q, c)
                    b_scan(b, q, c, 0, HS)
                    b_read(b, q, c)
                b_og(b, q)
                b_var(b)
                b_gn(b)
                b_x1(b, q)
                b_xhat(b)
                b_shift(b)
                b_y(b)

            def step(n, m, p):
                b, q = n - 1, 1 - p
                f_stats(n, m, p)
                b_outer(b, q, 0)
                f_norm(n, m, p)
                b_scan(b, q, 0, 0, HS)
                b_read(b, q, 0)
                f_vatt(n)
                b_outer(b, q, 1)
                f_max(n, 0)
                b_scan(b, q, 1, 0, 4)
                f_max(n, 1)
                f_probs(n, 0)
                b_scan(b, q, 1, 4, 8)
                f_max(n, 2)
                f_probs(n, 1)
                b_scan(b, q, 1, 8, 12)
                f_max(n, 3)
                f_probs(n, 2)
                b_scan(b, q, 1, 12, HS)
                f_probs(n, 3)
                b_read(b, q, 1)
                b_outer(b, q, 2)
                b_scan(b, q, 2, 0, HS)
                f_xin(n, m, p)
                b_read(b, q, 2)
                f_xhat(n, m, p)
                b_outer(b, q, 3)
                b_scan(b, q, 3, 0, HS)
                f_shift(n)
                b_read(b, q, 3)
                f_mix(n, 0)
                b_og(b, q)
                f_mix(n, 1)
                b_var(b)
                f_mix(n, 2)
                b_gn(b)
                f_mix(n, 3)
                b_x1(b, q)
                f_mix(n, 4)
                b_xhat(b)
                f_gate(n, m, p)
                b_shift(b)
                b_y(b)

            run(eng, step, front, back)

        @block.scalar
        def _(eng):
            sc = nc.scalar

            eng.wait_ge(setup_loaded[0], 32)

            def f_proj(n):
                for job, dst, bias in (("Mn", Mn, "bn"), ("Mm", Mm, "bm")):
                    eng.wait_ge(pe_front.sem, pe_front.count(job, n))
                    sc.activation(dst[:, :], bank_of(job)[:, :], ACT.Identity, bias=col(bias, 0)).then_inc(act_front.sem, 1)

            def f_exp(n, t):
                eng.wait_ge(dve_front.sem, dve_front.count(f"mx{t}", n))
                eng.wait_ge(pe_front.sem, pe_front.count(f"T3", n - 1))
                sc.activation(prob[:, t, :], bank_of(f"S{t}")[:, :], ACT.Exp, bias=nmax[:, t:t + 1],
                              accum_out=rsum[:, t:t + 1]).then_inc(act_front.sem, 1)

            def f_probT(n, s):
                eng.wait_ge(pe_front.sem, pe_front.count(f"T{s}", n))
                eng.wait_ge(pe_front.sem, pe_front.count("O", n - 1))
                sc.activation(probT[:, s, :], bank_of(f"T{s}")[:, :], ACT.Copy).then_inc(act_front.sem, 1)

            def f_xa(n):
                eng.wait_ge(pe_front.sem, pe_front.count("Tx", n))
                eng.wait_ge(dve_front.sem, dve_front.count("xx", n - 1))
                eng.wait_ge(pool_front.sem, pool_front.count("fg", n - 1))
                for c in range(C):
                    last = sc.activation(xa[:, c, 1:P + 1], bank_of("Tx")[:, c * P:(c + 1) * P], ACT.Identity,
                                         bias=col("ln1_b", c), scale=col("ln1_w", c))
                last.then_inc(act_front.sem, 1)

            def f_tx(n):
                eng.wait_ge(pe_front.sem, pe_front.count("W1", n))
                sc.activation(tx[:, :], bank_of("W1")[:, 0:P], ACT.Tanh)
                sc.activation(txg[:, :], bank_of("W1")[0:DM, P:2 * P], ACT.Tanh).then_inc(act_front.sem, 1)

            def f_v(n, m, p):
                eng.wait_ge(pe_front.sem, pe_front.count("Vp", n))
                if late(n):
                    eng.wait_ge(v_stored, 16 * n)
                sc.activation(vT[:, :, :], bank_of("Vp")[:, :].rearrange("p (c t) -> p c t", c=C),
                              ACT.Copy).then_inc(act_front.sem, 1)
                eng.wait_ge(act_front.sem, act_front.count("vT", n))
                if late(m):
                    eng.wait_ge(dve_back.sem, dve_back.count("a3", n - 2))
                eng.dma_start(v_dram[p].rearrange("(c e) t -> e c t", c=C), vT[:, :, :]).then_inc(v_stored, 16)
                eng.wait_ge(pe_front.sem, pe_front.count("TvN", n))
                if late(m):
                    eng.wait_ge(dve_back.sem, dve_back.count("o1", n - 2))
                sc.activation(vN[:, p, :], bank_of("TvN")[:, :], ACT.Copy).then_inc(act_front.sem, 1)

            def f_dt(n):
                eng.wait_ge(pe_front.sem, pe_front.count("D1", n))
                sc.activation(dt[:, :], bank_of("D1")[0:DD, 0:P], ACT.Tanh).then_inc(act_front.sem, 1)

            def f_w(n, m, p):
                eng.wait_ge(pe_front.sem, pe_front.count("D2", n))
                for c in range(C):
                    last = sc.activation(ez[:, c, :], bank_of("D2")[:, c * P:(c + 1) * P], ACT.Exp,
                                         bias=col("time_decay", c))
                last.then_inc(act_front.sem, 1)
                eng.wait_ge(act_front.sem, act_front.count("ez1", n))
                sc.activation(wT[:, p, :, :], ez[:, :, :], ACT.Exp, scale=-1.0).then_inc(act_front.sem, 1)

            def f_copyT(n, p, job, dst):
                eng.wait_ge(pe_front.sem, pe_front.count(job, n))
                sc.activation(dst[:, p, :, :], bank_of(job)[:, :].rearrange("p (c t) -> p c t", c=C),
                              ACT.Copy).then_inc(act_front.sem, 1)

            def f_th(n):
                eng.wait_ge(pe_front.sem, pe_front.count("G", n))
                sc.activation(th[:, :], bank_of("G")[:, :], ACT.Tanh, scale=0.5).then_inc(act_front.sem, 1)

            def b_oT(b):
                eng.wait_ge(pe_back.sem, pe_back.count("To", b))
                sc.activation(ogT[:, :, :], bank_of("To")[:, :].rearrange("p (c t) -> p c t", c=C),
                              ACT.Copy).then_inc(act_back.sem, 1)

            def b_xc2(b):
                eng.wait_ge(pe_back.sem, pe_back.count("Tx2", b))
                eng.wait_ge(dve_back.sem, dve_back.count("xr2", b - 1))
                for c in range(C):
                    last = sc.activation(xc2[:, c, 1:P + 1], bank_of("Tx2")[:, c * P:(c + 1) * P], ACT.Identity,
                                         bias=col("ln2_b", c), scale=col("ln2_w", c))
                last.then_inc(act_back.sem, 1)

            def b_ffn(b):
                eng.wait_ge(pe_back.sem, pe_back.count("FK", b))
                sc.activation(kr[:, :, :], bank_of("FK")[:, :].rearrange("p (c t) -> p c t", c=C),
                              ACT.Relu).then_inc(act_back.sem, 1)
                eng.wait_ge(pe_back.sem, pe_back.count("FR", b))
                eng.wait_ge(dve_back.sem, dve_back.count("y", b - 1))
                sc.activation(rr[:, :], bank_of("FR")[:, :], ACT.Tanh, scale=0.5).then_inc(act_back.sem, 1)

            def store(b):
                eng.wait_ge(pool_back.sem, pool_back.count("out", b))
                dst = out[b] if isinstance(b, int) else out[bass.ds(b, 1)].rearrange("o p f -> (o p) f")
                eng.dma_start(dst, ob[:, :]).then_inc(out_stored, 16)

            def front(n, m, p):
                f_proj(n)
                for t in range(C):
                    f_exp(n, t)
                for s in range(C):
                    f_probT(n, s)
                f_xa(n)
                f_tx(n)
                f_v(n, m, p)
                f_dt(n)
                f_w(n, m, p)
                f_copyT(n, p, "Kp", kT)
                f_copyT(n, p, "Rp", rT)
                f_th(n)

            def back(b, q):
                b_oT(b)
                b_xc2(b)
                b_ffn(b)
                store(b)

            def step(n, m, p):
                b = n - 1
                f_proj(n)
                for t in range(C):
                    f_exp(n, t)
                for s in range(C):
                    f_probT(n, s)
                f_xa(n)
                f_tx(n)
                f_v(n, m, p)
                f_dt(n)
                f_w(n, m, p)
                f_copyT(n, p, "Kp", kT)
                b_oT(b)
                f_copyT(n, p, "Rp", rT)
                f_th(n)
                b_xc2(b)
                b_ffn(b)
                store(b)

            run(eng, step, front, back)
            eng.wait_ge(out_stored, 16 * NB)

        @block.tensor
        def _(eng):
            pe = nc.tensor
            eng.wait_ge(setup_loaded[0], 32)
            pe.matmul(bank[0][:, 0:P], attw[:, 2, :], attw[:, 3, :], start=True, stop=True).then_inc(pe_setup, 1)
            eng.wait_ge(dve_setup, 1)
            pe.matmul(bank[1][:, 0:P], bl_rep[:, :], attw[:, 3, :], start=True, stop=True).then_inc(pe_setup, 1)
            eng.wait_ge(pool_const, 7)
            eng.wait_ge(dve_setup, 3)

            def proj_T(job, w, width, src):
                ps = bank_of(job)
                for o in range(C):
                    for c in range(C):
                        last = pe.matmul(ps[:, o * P:(o + 1) * P], w[:, c, o * P:(o + 1) * P], src[:, c, :],
                                         start=(c == 0), stop=(c == C - 1))
                return last

            def proj_N(job, w, src):
                for c in range(C):
                    last = pe.matmul(bank_of(job)[:, :], src[:, c, :], w[:, c, :], start=(c == 0), stop=(c == C - 1))
                return last

            def transposes(job, src):
                for c in range(C):
                    last = pe.transpose(bank_of(job)[:, c * P:(c + 1) * P], src(c), ident[:, :])
                return last

            def f_proj(n):
                eng.wait_ge(dve_front.sem, dve_front.count("xn", n))
                eng.wait_ge(*bank_free("Mn", n))
                pe.matmul(bank_of("Mn")[:, :], attw[:, 0, :], xn[:, :], start=True, stop=True).then_inc(pe_front.sem, 1)
                eng.wait_ge(dve_front.sem, dve_front.count("yn", n))
                eng.wait_ge(*bank_free("Mm", n))
                pe.matmul(bank_of("Mm")[:, :], attw[:, 1, :], yn[:, :], start=True, stop=True).then_inc(pe_front.sem, 1)

            def f_V(n, m, p):
                eng.wait_ge(*bank_free("V", n))
                for s in range(C):
                    last = pe.matmul(bank_of("V")[:, s * P:(s + 1) * P], xs[:, p, s * P:(s + 1) * P], wolT[:, :],
                                     start=True, stop=True)
                last.then_inc(pe_front.sem, 1)

            def f_S(n):
                eng.wait_ge(act_front.sem, act_front.count("Mm", n))
                for t in range(C):
                    eng.wait_ge(*bank_free(f"S{t}", n))
                    pe.matmul(bank_of(f"S{t}")[:, :], Mn[:, t * P:(t + 1) * P], Mm[:, :],
                              start=True, stop=True).then_inc(pe_front.sem, 1)

            def f_T(n):
                eng.wait_ge(dve_front.sem, dve_front.count("pn3", n))
                for s in range(C):
                    eng.wait_ge(*bank_free(f"T{s}", n))
                    transposes(f"T{s}", lambda t: prob[:, t, s * P:(s + 1) * P]).then_inc(pe_front.sem, 1)

            def f_O(n):
                eng.wait_ge(*bank_free("O", n))
                for s in range(C):
                    eng.wait_ge(act_front.sem, act_front.count(f"T{s}", n))
                    if s == 0:
                        eng.wait_ge(dve_front.sem, dve_front.count("vatt", n))
                    last = pe.matmul(bank_of("O")[:, :], vT_att[:, s, :], probT[:, s, :],
                                     start=(s == 0), stop=(s == C - 1))
                last.then_inc(pe_front.sem, 1)

            def f_Tx(n):
                eng.wait_ge(dve_front.sem, dve_front.count("xhat", n))
                eng.wait_ge(*bank_free("Tx", n))
                transposes("Tx", lambda c: xhat[:, c * P:(c + 1) * P]).then_inc(pe_front.sem, 1)

            def f_W1(n):
                if isinstance(n, int) and n == 0:
                    eng.wait_ge(setup_loaded[1], 80)
                eng.wait_ge(dve_front.sem, dve_front.count("xx", n))
                eng.wait_ge(*bank_free("W1", n))
                ps = bank_of("W1")
                for c in range(C):
                    pe.matmul(ps[:, 0:P], w1[:, c, 0:P], xx[:, c, :], start=(c == 0), stop=(c == C - 1))
                for c in range(C):
                    last = pe.matmul(ps[0:DM, P:2 * P], w1[:, c, P:P + DM], xx[:, c, :],
                                     start=(c == 0), stop=(c == C - 1))
                last.then_inc(pe_front.sem, 1)

            def f_M(n, f):
                i = MIX.index(f)
                eng.wait_ge(act_front.sem, act_front.count("tx", n))
                eng.wait_ge(*bank_free(f"M{f}", n))
                w, x_ = (w2g[:, :], txg[:, :]) if f == "g" else (w2[DM * i:DM * i + DM, :], tx[DM * i:DM * i + DM, :])
                for c in range(C):
                    last = pe.matmul(bank_of(f"M{f}")[:, c * P:(c + 1) * P], w[:, c * P:(c + 1) * P], x_,
                                     start=True, stop=True)
                last.then_inc(pe_front.sem, 1)

            def xf_of(f):
                return xf[:, ORDER.index(f) % 2, :, :]

            def f_P(n, f, job, name):
                if isinstance(n, int) and n == 0:
                    eng.wait_ge(setup_loaded[2], 16 * len(BIG))
                eng.wait_ge(pool_front.sem, pool_front.count(f"f{f}", n))
                eng.wait_ge(*bank_free(job, n))
                if f == "g":
                    proj_N(job, W[name], xf_of(f)).then_inc(pe_front.sem, 1)
                else:
                    proj_T(job, W[name], E, xf_of(f)).then_inc(pe_front.sem, 1)

            def f_TvN(n):
                eng.wait_ge(act_front.sem, act_front.count("vT", n))
                eng.wait_ge(*bank_free("TvN", n))
                transposes("TvN", lambda c: vT[:, c, :]).then_inc(pe_front.sem, 1)

            def f_D1(n):
                eng.wait_ge(pool_front.sem, pool_front.count("fw", n))
                eng.wait_ge(*bank_free("D1", n))
                for c in range(C):
                    last = pe.matmul(bank_of("D1")[0:DD, 0:P], tw1[:, c, :], xf_of("w")[:, c, :],
                                     start=(c == 0), stop=(c == C - 1))
                last.then_inc(pe_front.sem, 1)

            def f_D2(n):
                eng.wait_ge(act_front.sem, act_front.count("dt", n))
                eng.wait_ge(*bank_free("D2", n))
                for c in range(C):
                    last = pe.matmul(bank_of("D2")[:, c * P:(c + 1) * P], tw2[:, c * P:(c + 1) * P], dt[:, :],
                                     start=True, stop=True)
                last.then_inc(pe_front.sem, 1)

            def b_C(b):
                eng.wait_ge(pool_back.sem, pool_back.count("rku", b))
                eng.wait_ge(*bank_free("C", b))
                for c in range(C):
                    last = pe.matmul(bank_of("C")[:, c * HC:(c + 1) * HC], rku[:, c, :], head_sum[:, :],
                                     start=True, stop=True)
                last.then_inc(pe_back.sem, 1)

            def b_red(b, c):
                eng.wait_ge(dve_back.sem, dve_back.count(f"q{c}", b))
                if c == 0:
                    eng.wait_ge(dve_back.sem, dve_back.count("o2", b - 1))
                o = bank[WKV_BANK][:, c * P:(c + 1) * P].rearrange("p (h j) -> p h j", j=HS)
                for j in range(HS):
                    last = pe.matmul(o[:, :, j], S[:, c % 2, j, :], head_sum[:, :], start=True, stop=True)
                last.then_inc(pe_back.sem, 1)

            def b_To(b):
                eng.wait_ge(dve_back.sem, dve_back.count("o5", b))
                eng.wait_ge(*bank_free("To", b))
                transposes("To", lambda c: og[:, c * P:(c + 1) * P]).then_inc(pe_back.sem, 1)

            def b_Wo(b):
                eng.wait_ge(act_back.sem, act_back.count("oT", b))
                eng.wait_ge(*bank_free("Wo", b))
                proj_N("Wo", W["Wo"], ogT).then_inc(pe_back.sem, 1)

            def b_Tx2(b):
                eng.wait_ge(dve_back.sem, dve_back.count("xh", b))
                eng.wait_ge(*bank_free("Tx2", b))
                transposes("Tx2", lambda c: xhat2[:, c * P:(c + 1) * P]).then_inc(pe_back.sem, 1)

            def b_FK(b):
                eng.wait_ge(dve_back.sem, dve_back.count("xk2", b))
                eng.wait_ge(*bank_free("FK", b))
                proj_T("FK", W["Wfk"], E, xk2).then_inc(pe_back.sem, 1)

            def b_FR(b):
                eng.wait_ge(dve_back.sem, dve_back.count("xr2", b))
                eng.wait_ge(*bank_free("FR", b))
                proj_N("FR", W["Wfr"], xr2).then_inc(pe_back.sem, 1)

            def b_FV(b):
                eng.wait_ge(pool_back.sem, pool_back.count("kk", b))
                eng.wait_ge(*bank_free("FV", b))
                proj_N("FV", W["Wfv"], kk).then_inc(pe_back.sem, 1)

            def front(n, m, p):
                f_proj(n)
                f_V(n, m, p)
                f_S(n)
                f_T(n)
                f_O(n)
                f_Tx(n)
                f_W1(n)
                f_M(n, "v")
                f_M(n, "w")
                f_P(n, "v", "Vp", "Wv")
                f_TvN(n)
                f_D1(n)
                f_M(n, "k")
                f_D2(n)
                f_P(n, "k", "Kp", "Wk")
                f_M(n, "r")
                f_P(n, "r", "Rp", "Wr")
                f_M(n, "g")
                f_P(n, "g", "G", "Wg")

            def back(b, q):
                b_C(b)
                for c in range(C):
                    b_red(b, c)
                b_To(b)
                b_Wo(b)
                b_Tx2(b)
                b_FK(b)
                b_FR(b)
                b_FV(b)

            def step(n, m, p):
                b = n - 1
                b_C(b)
                f_proj(n)
                f_V(n, m, p)
                b_red(b, 0)
                f_S(n)
                b_red(b, 1)
                f_T(n)
                f_O(n)
                b_red(b, 2)
                f_Tx(n)
                f_W1(n)
                f_M(n, "v")
                b_red(b, 3)
                f_M(n, "w")
                f_P(n, "v", "Vp", "Wv")
                f_TvN(n)
                f_D1(n)
                f_M(n, "k")
                f_D2(n)
                f_P(n, "k", "Kp", "Wk")
                f_M(n, "r")
                b_To(b)
                f_P(n, "r", "Rp", "Wr")
                f_M(n, "g")
                b_Wo(b)
                f_P(n, "g", "G", "Wg")
                b_Tx2(b)
                b_FK(b)
                b_FR(b)
                b_FV(b)

            run(eng, step, front, back)


def kernel(**inputs):
    import numpy as np
    import concourse.bacc as bacc
    from concourse.bass_utils import run_bass_kernel_spmd

    a = {k.replace("_xattn_", "_"): np.asarray(v) for k, v in inputs.items()}

    def chunked(w):
        return np.ascontiguousarray(w.reshape(C, P, -1).transpose(1, 0, 2))

    def column(v):
        return v.reshape(C, P).T

    ctx = a["ctx_2048"]
    one = lambda v: v.reshape(P, 1)
    u = a["L1_u"].reshape(E)
    params = np.concatenate(
        [column(a["L1_" + k]) for k in ("ln1_w", "ln1_b", "ln2_w", "ln2_b", "maa_x", "time_decay",
                                         "ffn_maa_k", "ffn_maa_r")]
        + [column(u)] + [column(a["L1_maa_stack"][0, f]) for f in range(5)]
        + [one(a["L0_" + k]) for k in ("bn", "bm", "bl", "bo")], axis=1)
    rows = ctx[:, 0:2, :].reshape(NB, 2, C, P).transpose(0, 3, 1, 2).reshape(NB, P, 2 * C)
    s0 = ctx[:, 2:2 + HS, :].reshape(NB, C, P, HS).transpose(0, 2, 1, 3).reshape(NB, P, C * HS)
    arrays = {
        "x_c": a["x"],
        "x_s": ctx,
        "state": np.concatenate([rows, s0], axis=2),
        "params": params,
        "att_w": np.stack([a["L0_Wn"].T, a["L0_Wm"].T, a["L0_Wl"], a["L0_Wo"].T], axis=1),
        "big_w": np.stack([chunked(a["L1_" + k].T) for k in BIG]),
        "maa_w1": chunked(a["L1_maa_w1"]),
        "maa_w2": a["L1_maa_w2"].reshape(5 * DM, E),
        "td_w1": chunked(a["L1_td_w1"]),
        "td_w2": a["L1_td_w2"],
        "gn": np.stack([a["L1_gn_w"], a["L1_gn_b"]]),
    }
    arrays = {k: np.ascontiguousarray(v) for k, v in arrays.items()}
    nc = bacc.Bacc("TRN2", target_bir_lowering=False, num_devices=1)
    args = [nc.dram_tensor(k, v.shape, mybir.dt.from_np(v.dtype), kind="ExternalInput").ap()
            for k, v in arrays.items()]
    args.append(nc.dram_tensor("out", (NB, P, E), F32, kind="ExternalOutput").ap())
    args.append(nc.dram_tensor("v_dram", (2, E, P), F32).ap())
    build(nc, *args)
    result = run_bass_kernel_spmd(nc, [arrays], core_ids=[0])
    return result.results[0]["out"]
```

```python
from contextlib import ExitStack

import concourse.bass as bass
from concourse import mybir

F32 = mybir.dt.float32
ALU = mybir.AluOpType
ACT = mybir.ActivationFunctionType
X = mybir.AxisListType.X

NB = 32
P = 128
E = 512
C = E // P
HS = 16
H = E // HS
HC = H // C
UJ = 8
U = C * HS // UJ
LAG = {"att": 0, "mid": 1, "wkv": 2, "tail": 3, "fin": 4}
STEPS = NB + 4
FIRST = 5
DM = 32
DD = 64
EPS = 1e-5
MIX = "kwvrg"
ORDER = "vwkrg"

COLS = {"ln1_w": 0, "ln1_b": 4, "ln2_w": 8, "ln2_b": 12, "maa_x": 16, "time_decay": 20,
        "ffn_maa_k": 24, "ffn_maa_r": 28, "u": 32, "maa_stack": 36, "bn": 56, "bm": 57, "bl": 58, "bo": 59}
NPAR = 60
BIG = ["Wv", "Wk", "Wr", "Wg", "Wo", "Wfk", "Wfr", "Wfv"]
ST0, ST1, STS, NST = 0, C, 2 * C, 2 * C + C * HS


class Steps:

    def __init__(self, sem, labels):
        self.sem, self.at = sem, {x: k for k, x in enumerate(labels.split())}

    def count(self, label, n):
        if isinstance(n, int) and n < 0:
            return 0
        return n * len(self.at) + self.at[label] + 1


def held(eng, register, value):
    if isinstance(value, int):
        return value
    eng.reg_mov(register, value)
    return register


def run(eng, step):
    def stages(s, m_of):
        return {k: (s - lag, *m_of(lag)) for k, lag in LAG.items()
                if not isinstance(s, int) or 0 <= s - lag < NB}

    def peeled(s):
        step(s, stages(s, lambda lag: ((s - lag) // 2, (s - lag) % 2)))

    for s in range(FIRST):
        peeled(s)
    pairs = (NB - FIRST) // 2
    with eng.Fori(0, pairs) as i:
        for k in (FIRST, FIRST + 1):
            step(i * 2 + k, stages(i * 2 + k, lambda lag: (i + (k - lag) // 2, (k - lag) % 2)))
    for s in range(FIRST + 2 * pairs, STEPS):
        peeled(s)


FRONT_JOBS = [(j, st) for j, st in (x.split(":") for x in (
    "Tx:mid Mn:att Mm:att V:att W1:mid S0:att S1:att Mv:mid Mw:mid S2:att S3:att Mk:mid Vp:mid D1:mid "
    "Kp:mid Mr:mid D2:mid T0:att T1:att T2:att T3:att Mg:mid Rp:mid O:att G:mid").split())]
BACK_JOBS = [(j, st) for j, st in (x.split(":") for x in
             "C:tail FR:fin To:tail FV:fin Tg:tail Wo:tail Tx2:tail FK:tail".split())]
FRONT_BANKS, BACK_BANKS, WKV_BANKS = [0, 1, 2, 3], [6, 7], [4, 5]


def build(nc, x_c, x_s, state, params, att_w, big_w, maa_w1, maa_w2, td_w1, td_w2, gn, out, v_dram):
    with ExitStack() as ctx:
        def sb(name, shape):
            return ctx.enter_context(nc.sbuf_tensor(name, shape, F32))

        def sem(name):
            return ctx.enter_context(nc.semaphore(name))

        bank = [ctx.enter_context(nc.psum_tensor(f"bank{i}", [P, E], F32)) for i in range(8)]

        ident = sb("ident", [P, P])
        head_rep = sb("head_rep", [P, P])
        slide = sb("slide", [P, P + HS])
        mhalf = sb("mhalf", [P, H])
        par = sb("par", [P, NPAR])
        attw = sb("attw", [P, 4, P])
        wolT = sb("wolT", [P, P])
        vbias = sb("vbias", [P, P])
        W = {name: sb(name, [P, C, E]) for name in BIG}
        w1 = sb("w1", [P, C, 5 * DM])
        w2 = sb("w2", [P, E])
        w2g = sb("w2g", [DM, E])
        tw1 = sb("tw1", [P, C, DD])
        tw2 = sb("tw2", [DD, E])
        gnw = sb("gnw", [P, 2, E])

        xc = sb("xc", [P, 2, E])
        xs = sb("xs", [P, 2, E])
        st6 = sb("st6", [P, 3, 6])
        mv = sb("mv", [P, 3, 2])
        ve = sb("ve", [P, 4])
        rstd = sb("rstd", [P, 4])
        Mn = sb("Mn", [P, E])
        Mm = sb("Mm", [P, E])
        v_att = sb("v_att", [P, C, P])
        prob = sb("prob", [P, C, E])
        probT = sb("probT", [P, C, E])
        nmax = sb("nmax", [P, C])
        rsum = sb("rsum", [P, C])
        rinv = sb("rinv", [P, C])
        xhat = sb("xhat", [P, E])
        xin = sb("xin", [P, 2, E])
        st1 = sb("st1", [P, 2, C])
        xa = sb("xa", [P, C, P + 1])
        sx = sb("sx", [P, C, P])
        xx = sb("xx", [P, C, P])
        tx = sb("tx", [P, P])
        txg = sb("txg", [DM, P])
        mt = sb("mt", [P, 2, C, P])
        xf = sb("xf", [P, 2, C, P])
        dt = sb("dt", [DD, P])
        ez = sb("ez", [P, C, P])
        th = sb("th", [P, E])
        xres = sb("xres", [P, 2, E])
        kT = sb("kT", [P, 2, C, P])
        rT = sb("rT", [P, 2, C, P])
        wT = sb("wT", [P, 2, C, P])
        vT = sb("vT", [P, 2, C, P])
        gN = sb("gN", [P, 2, E])
        s0 = sb("s0", [P, 2, C * HS])
        rku = sb("rku", [P, C, P])
        vrep = sb("vrep", [P, 2, UJ, P])
        S = sb("S", [P, 2, UJ, P])
        st0 = sb("st0", [P, 2, C])
        og = sb("og", [P, E])
        oc = sb("oc", [P, E])
        sq = sb("sq", [P, E])
        gw = sb("gw", [P, E])
        gb = sb("gb", [P, E])
        hsum = sb("hsum", [P, 2, H])
        hve = sb("hve", [P, H])
        hrs = sb("hrs", [P, H])
        ogT = sb("ogT", [P, C, P])
        x1 = sb("x1", [P, E])
        st62 = sb("st62", [P, 6])
        mv2 = sb("mv2", [P, 2])
        ve2 = sb("ve2", [P, 1])
        rstd2 = sb("rstd2", [P, 1])
        xc2 = sb("xc2", [P, C, P + 1])
        sx2 = sb("sx2", [P, C, P])
        xr2 = sb("xr2", [P, C, P])
        kk = sb("kk", [P, C, P])
        rr = sb("rr", [P, E])

        xn = prob[:, 0, :]
        yn = prob[:, 1, :]
        bl_rep = prob[:, 2, 0:P]
        xhat2 = sq
        xk2 = gw[:, :].rearrange("p (c t) -> p c t", c=C)

        def by_chunk(ap):
            return ap.rearrange("p (c t) -> p c t", c=C)

        def col(name, c, f=0):
            k = COLS[name] + C * f + c
            return par[:, k:k + 1]

        setup_loaded = [sem(f"setup_loaded{i}") for i in range(4)]
        x_loaded = [sem(f"x_loaded{i}") for i in range(2)]
        st1_loaded = [sem(f"st1_loaded{i}") for i in range(2)]
        s0_loaded = [sem(f"s0_loaded{i}") for i in range(2)]
        st0_loaded = [sem(f"st0_loaded{i}") for i in range(2)]
        vrep_loaded = [sem(f"vrep_loaded{i}") for i in range(2)]
        v_stored = sem("v_stored")
        out_stored = sem("out_stored")
        pool_const = sem("pool_const")
        pe_setup = sem("pe_setup")
        dve_setup = sem("dve_setup")

        def units(text):
            return " ".join(f"{x}{u}" for u in range(U) for x in text.split())

        dve_att = Steps(sem("dve_att"), "stats aggr xn yn vatt mx0 mx1 ri0 ri1 mx2 mx3 ri2 ri3 xin xst xag xhat")
        dve_mid = Steps(sem("dve_mid"), "sx xx mv mw mk mr mg g")
        dve_wkv = Steps(sem("dve_wkv"), units("a s q"))
        dve_tail = Steps(sem("dve_tail"), "o1 o2 sum oc var o3 o4 o5 x1 st ag xh sx2 xk2 xr2")
        dve_fin = Steps(sem("dve_fin"), "y")
        act_att = Steps(sem("act_att"), "Mn Mm p0 p1 n0 n1 p2 p3 n2 n3 T0 T1 T2 T3")
        act_mid = Steps(sem("act_mid"), "xa tx vT dt k ez w r th")
        act_tail = Steps(sem("act_tail"), "oT xc2")
        act_fin = Steps(sem("act_fin"), "kr thr rr")
        pool_att = Steps(sem("pool_att"), "ve rstd ve1 rstd1")
        pool_mid = Steps(sem("pool_mid"), "xa0 fv fw fk fr fg xres")
        pool_wkv = Steps(sem("pool_wkv"), "z0 z1 rk rku z2 z3 z4 z5 z6 z7")
        pool_tail = Steps(sem("pool_tail"), "gw gb sq hve hrs ve2 rstd2 xc20")
        pool_fin = Steps(sem("pool_fin"), "kk out")
        pe_att = Steps(sem("pe_att"), "Mn Mm V S0 S1 S2 S3 T0 T1 T2 T3 O")
        pe_mid = Steps(sem("pe_mid"), "Tx W1 Mv Mw Mk Vp D1 Kp Mr D2 Mg Rp G")
        pe_wkv = Steps(sem("pe_wkv"), units("r"))
        pe_tail = Steps(sem("pe_tail"), "C To Tg Wo Tx2 FK")
        pe_fin = Steps(sem("pe_fin"), "FR FV")

        reader = {"Mn": (act_att, "Mn"), "Mm": (act_att, "Mm"), "V": (dve_att, "vatt"), "O": (dve_att, "xin"),
                  "Tx": (act_mid, "xa"), "W1": (act_mid, "tx"), "Vp": (act_mid, "vT"), "D1": (act_mid, "dt"),
                  "D2": (act_mid, "ez"), "Kp": (act_mid, "k"), "Rp": (act_mid, "r"), "G": (dve_mid, "g"),
                  "C": (dve_tail, "o1"), "To": (dve_tail, "oc"), "Tg": (act_tail, "oT"), "Wo": (dve_tail, "x1"),
                  "Tx2": (act_tail, "xc2"), "FK": (act_fin, "kr"), "FR": (act_fin, "thr"), "FV": (dve_fin, "y")}
        reader.update({f"S{i}": (act_att, f"p{i}") for i in range(C)})
        reader.update({f"T{i}": (act_att, f"T{i}") for i in range(C)})
        reader.update({f"M{f}": (dve_mid, f"m{f}") for f in MIX})

        def ring_of(job):
            for jobs, banks in ((FRONT_JOBS, FRONT_BANKS), (BACK_JOBS, BACK_BANKS)):
                names = [j for j, _ in jobs]
                if job in names:
                    return jobs, banks, names.index(job)

        def bank_of(job):
            _, banks, q = ring_of(job)
            return bank[banks[q % len(banks)]]

        def bank_free(job, n):
            jobs, banks, q = ring_of(job)
            s = n + LAG[jobs[q][1]]
            while True:
                q -= len(banks)
                if q < 0:
                    q += len(banks)
                    while q + len(banks) < len(jobs):
                        q += len(banks)
                    s = s - 1
                name, stage = jobs[q]
                steps, label = reader[name]
                before = s - LAG[stage]
                if isinstance(before, int) and s >= 0 and not 0 <= before < NB:
                    continue
                return steps.sem, steps.count(label, before)

        block = ctx.enter_context(nc.Block())

        @block.sync
        def _(sp):
            regs = [sp.alloc_register(f"sync_wait{i}") for i in range(2)]
            sp.dma_start(attw[:, :, :], att_w).then_inc(setup_loaded[0], 16)
            sp.dma_start(par[:, :], params).then_inc(setup_loaded[0], 16)

            def of(tensor, n):
                return tensor[n] if isinstance(n, int) else tensor[bass.ds(n, 1)].rearrange("o p f -> (o p) f")

            def load_x(n, p):
                v0 = held(sp, regs[0], dve_att.count("xin", n - 2))
                v1 = held(sp, regs[1], pe_att.count("V", n - 2))
                sp.wait_ge(setup_loaded[0], 32)
                sp.wait_ge(dve_att.sem, v0)
                sp.wait_ge(pe_att.sem, v1)
                sp.dma_start(xc[:, p, :], of(x_c, n)).then_inc(x_loaded[p], 16)
                sp.dma_start(xs[:, p, :], of(x_s, n)).then_inc(x_loaded[p], 16)

            def load_st1(n, p):
                v0 = held(sp, regs[0], pool_mid.count("xa0", n - 2))
                sp.wait_ge(setup_loaded[0], 32)
                sp.wait_ge(pool_mid.sem, v0)
                sp.dma_start(st1[:, p, :], of(state, n)[:, ST1:ST1 + C]).then_inc(st1_loaded[p], 16)

            def load_s0(n, p):
                v0 = held(sp, regs[0], dve_wkv.count(f"s{U - 1}", n - 2))
                v1 = held(sp, regs[1], pool_wkv.count(f"z{U - 1}", n - 2))
                sp.wait_ge(setup_loaded[0], 32)
                sp.wait_ge(dve_wkv.sem, v0)
                sp.wait_ge(pool_wkv.sem, v1)
                sp.dma_start(s0[:, p, :], of(state, n)[:, STS:NST]).then_inc(s0_loaded[p], 16)

            def load_st0(n, p):
                v0 = held(sp, regs[0], pool_tail.count("xc20", n - 2))
                sp.wait_ge(setup_loaded[0], 32)
                sp.wait_ge(pool_tail.sem, v0)
                sp.dma_start(st0[:, p, :], of(state, n)[:, ST0:ST0 + C]).then_inc(st0_loaded[p], 16)

            def load_vrep(n, p, u):
                src = v_dram[p].rearrange("(c h j) t -> c h (j t)", c=C, h=HC)
                c, j0 = u // 2, UJ * (u % 2)
                v0 = held(sp, regs[0], 16 * (n + 1))
                v1 = held(sp, regs[1], dve_wkv.count(f"s{(u - 2) % U}", n if u >= 2 else n - 1))
                sp.wait_ge(setup_loaded[0], 32)
                sp.wait_ge(v_stored, v0)
                sp.wait_ge(dve_wkv.sem, v1)
                sp.dma_start(vrep[:, u % 2, :, :].rearrange("p j t -> p (j t)"),
                             src[c][:, j0 * P:(j0 + UJ) * P].unsqueeze(1).broadcast_to([HC, HS, UJ * P]))\
                    .then_inc(vrep_loaded[u % 2], 16)

            load_x(0, 0)
            sp.dma_start(w1[:, :, :], maa_w1).then_inc(setup_loaded[1], 16)
            sp.dma_start(w2[:, :], maa_w2[0:P, :]).then_inc(setup_loaded[1], 16)
            sp.dma_start(w2g[:, :], maa_w2[P:P + DM, :]).then_inc(setup_loaded[1], 16)
            sp.dma_start(tw1[:, :, :], td_w1).then_inc(setup_loaded[1], 16)
            sp.dma_start(tw2[:, :], td_w2).then_inc(setup_loaded[1], 16)
            sp.dma_start(gnw[:, :, :], gn.unsqueeze(0).broadcast_to([P, 2, E])).then_inc(setup_loaded[3], 16)
            for k, name in enumerate(BIG):
                sp.dma_start(W[name][:, :, :], big_w[k]).then_inc(setup_loaded[2], 16)

            def step(s, on):
                a, m, w, t = (on.get(k) for k in ("att", "mid", "wkv", "tail"))
                if w:
                    load_vrep(w[0], w[2], 0)
                    load_vrep(w[0], w[2], 1)
                if not isinstance(s, int) or s + 1 < NB:
                    load_x(a[0] + 1, 1 - a[2])
                if a:
                    load_st1(a[0], a[2])
                if m:
                    load_s0(m[0], m[2])
                if w:
                    load_st0(w[0], w[2])
                    for u in range(2, U):
                        load_vrep(w[0], w[2], u)

            run(sp, step)

        @block.gpsimd
        def _(eng):
            po = nc.gpsimd
            regs = [eng.alloc_register(f"pool_wait{i}") for i in range(3)]
            po.memset(ident[:, :], 0.0).then_inc(pool_const, 1)
            po.memset(head_rep[:, :], 1.0).then_inc(pool_const, 1)
            po.memset(slide[:, :], 0.0).then_inc(pool_const, 1)
            po.memset(mhalf[:, :], -0.5).then_inc(pool_const, 1)
            eng.wait_ge(pool_const, 4)
            po.affine_select(out=ident[:, :], in_=ident[:, :], compare_op=ALU.not_equal, fill=1.0, base=0,
                             pattern=[[-1, P]], channel_multiplier=1).then_inc(pool_const, 1)
            rep = head_rep[:, :].rearrange("p (h j) -> p h j", j=HS)
            po.affine_select(out=rep, in_=rep, compare_op=ALU.is_ge, fill=0.0, base=0,
                             pattern=[[-HS, HC], [0, HS]], channel_multiplier=1).then_inc(pool_const, 1)
            eng.wait_ge(pool_const, 6)
            po.affine_select(out=rep, in_=rep, compare_op=ALU.is_ge, fill=0.0, base=HS - 1,
                             pattern=[[HS, HC], [0, HS]], channel_multiplier=-1).then_inc(pool_const, 1)
            eng.wait_ge(pool_const, 7)
            po.tensor_copy(slide[:, HS - 1:HS - 1 + P].rearrange("p (h j) -> p h j", j=HS)[:, :, 0],
                           rep[:, :, 0]).then_inc(pool_const, 1)
            eng.wait_ge(setup_loaded[3], 16)
            po.tensor_scalar(gnw[:, :, :], gnw[:, :, :], 0.5, None, ALU.mult).then_inc(pool_const, 1)
            eng.wait_ge(pool_const, 9)

            def rstd_of(res, var, tmp, scale, var_sem, var_count, own, own_label, n):
                v0 = held(eng, regs[0], var_count)
                eng.wait_ge(pool_const, 9)
                eng.wait_ge(var_sem, v0)
                po.tensor_scalar(tmp, var, scale, EPS, ALU.mult, ALU.add).then_inc(own.sem, 1)
                eng.wait_ge(own.sem, own.count(own_label, n))
                po.tensor_tensor(res, tmp, mhalf[:, 0:tmp.shape[1]], ALU.pow).then_inc(own.sem, 1)

            def att_rstd(n, m, p):
                rstd_of(rstd[:, 0:2], mv[:, 0:2, 1], ve[:, 0:2], 1.0,
                        dve_att.sem, dve_att.count("aggr", n), pool_att, "ve", n)

            def att_rstd1(n, m, p):
                rstd_of(rstd[:, 2:3], mv[:, 2:3, 1], ve[:, 2:3], 1.0,
                        dve_att.sem, dve_att.count("xag", n), pool_att, "ve1", n)

            def mid_xa0(n, m, p):
                v0 = held(eng, regs[0], 16 * (m + 1))
                v1 = held(eng, regs[1], dve_mid.count("xx", n - 1))
                v2 = held(eng, regs[2], pool_mid.count("fg", n - 1))
                eng.wait_ge(pool_const, 9)
                eng.wait_ge(st1_loaded[p], v0)
                eng.wait_ge(dve_mid.sem, v1)
                eng.wait_ge(pool_mid.sem, v2)
                po.tensor_copy(xa[:, :, 0], st1[:, p, :]).then_inc(pool_mid.sem, 1)

            def mid_add(n, m, p, i):
                f, b = ORDER[i], i % 2
                user = {"v": "G", "w": "Rp", "k": "Vp", "r": "D1", "g": "Kp"}[f]
                eng.wait_ge(dve_mid.sem, dve_mid.count(f"m{f}", n))
                eng.wait_ge(pe_mid.sem, pe_mid.count(user, n - 1 if i < 2 else n))
                po.tensor_tensor(xf[:, b, :, :], mt[:, b, :, :], xa[:, :, 1:P + 1],
                                 ALU.add).then_inc(pool_mid.sem, 1)

            def mid_xres(n, m, p):
                v0 = held(eng, regs[0], dve_tail.count("x1", n - 2))
                eng.wait_ge(pool_const, 9)
                eng.wait_ge(dve_tail.sem, v0)
                po.tensor_copy(xres[:, p, :], xin[:, p, :]).then_inc(pool_mid.sem, 1)

            def wkv_rku(n, m, p):
                eng.wait_ge(act_mid.sem, act_mid.count("r", n))
                eng.wait_ge(pe_tail.sem, pe_tail.count("C", n - 1))
                po.tensor_tensor(rku[:, :, :], rT[:, p, :, :], kT[:, p, :, :], ALU.mult).then_inc(pool_wkv.sem, 1)
                eng.wait_ge(pool_wkv.sem, pool_wkv.count("rk", n))
                u_b = par[:, COLS["u"]:COLS["u"] + C].unsqueeze(2).broadcast_to([P, C, P])
                po.tensor_tensor(rku[:, :, :], rku[:, :, :], u_b, ALU.mult).then_inc(pool_wkv.sem, 1)

            def wkv_s0(n, m, p, u):
                v0 = held(eng, regs[0], 16 * (m + 1))
                v1 = held(eng, regs[1], pe_wkv.count(f"r{(u - 2) % U}", n if u >= 2 else n - 1))
                eng.wait_ge(pool_const, 9)
                eng.wait_ge(s0_loaded[p], v0)
                eng.wait_ge(pe_wkv.sem, v1)
                po.tensor_copy(S[:, u % 2, :, 0], s0[:, p, UJ * u:UJ * u + UJ]).then_inc(pool_wkv.sem, 1)

            def tail_gate(n, m, p):
                eng.wait_ge(dve_mid.sem, dve_mid.count("g", n))
                eng.wait_ge(pe_tail.sem, pe_tail.count("FK", n - 1))
                po.tensor_tensor(gw[:, :], gN[:, p, :], gnw[:, 0, :], ALU.mult).then_inc(pool_tail.sem, 1)
                po.tensor_tensor(gb[:, :], gN[:, p, :], gnw[:, 1, :], ALU.mult).then_inc(pool_tail.sem, 1)

            def tail_sq(n, m, p):
                eng.wait_ge(dve_tail.sem, dve_tail.count("oc", n))
                eng.wait_ge(pe_tail.sem, pe_tail.count("Tx2", n - 1))
                po.tensor_tensor(sq[:, :], oc[:, :], oc[:, :], ALU.mult).then_inc(pool_tail.sem, 1)

            def tail_hrs(n, m, p):
                rstd_of(hrs[:, :], hsum[:, 1, :], hve[:, :], 1.0 / HS,
                        dve_tail.sem, dve_tail.count("var", n), pool_tail, "hve", n)

            def tail_rstd(n, m, p):
                rstd_of(rstd2[:, :], mv2[:, 1:2], ve2[:, :], 1.0,
                        dve_tail.sem, dve_tail.count("ag", n), pool_tail, "ve2", n)

            def tail_xc20(n, m, p):
                v0 = held(eng, regs[0], 16 * (m + 1))
                v1 = held(eng, regs[1], dve_tail.count("xr2", n - 1))
                eng.wait_ge(pool_const, 9)
                eng.wait_ge(st0_loaded[p], v0)
                eng.wait_ge(dve_tail.sem, v1)
                po.tensor_copy(xc2[:, :, 0], st0[:, p, :]).then_inc(pool_tail.sem, 1)

            def fin_kk(n, m, p):
                eng.wait_ge(act_fin.sem, act_fin.count("kr", n))
                po.tensor_tensor(kk[:, :, :], kk[:, :, :], kk[:, :, :], ALU.mult).then_inc(pool_fin.sem, 1)

            def fin_out(n, m, p):
                eng.wait_ge(dve_fin.sem, dve_fin.count("y", n))
                po.tensor_tensor(rr[:, :], rr[:, :], x1[:, :], ALU.add).then_inc(pool_fin.sem, 1)

            def step(s, on):
                a, m, w, t, f = (on.get(k) for k in LAG)
                if f: fin_kk(*f)
                if w: wkv_s0(*w, 0)
                if a: att_rstd(*a)
                if m: mid_xa0(*m)
                if w: wkv_s0(*w, 1)
                if t: tail_gate(*t)
                if w: wkv_rku(*w)
                if w: wkv_s0(*w, 2)
                if t: tail_sq(*t)
                if w: wkv_s0(*w, 3)
                if t: tail_hrs(*t)
                if m: mid_add(*m, 0)
                if w: wkv_s0(*w, 4)
                if m: mid_add(*m, 1)
                if f: fin_out(*f)
                if m: mid_add(*m, 2)
                if w: wkv_s0(*w, 5)
                if m: mid_add(*m, 3)
                if w: wkv_s0(*w, 6)
                if t: tail_rstd(*t)
                if t: tail_xc20(*t)
                if m: mid_add(*m, 4)
                if w: wkv_s0(*w, 7)
                if m: mid_xres(*m)
                if a: att_rstd1(*a)

            run(eng, step)

        @block.vector
        def _(eng):
            ve_ = nc.vector
            regs = [eng.alloc_register("vector_wait")]
            eng.wait_ge(setup_loaded[0], 32)
            ve_.tensor_copy(bl_rep, par[:, COLS["bl"]:COLS["bl"] + 1].broadcast_to([P, P])).then_inc(dve_setup, 1)
            eng.wait_ge(pe_setup, 2)
            ve_.tensor_copy(wolT[:, :], bank[0][:, 0:P]).then_inc(dve_setup, 1)
            ve_.tensor_copy(vbias[:, :], bank[1][:, 0:P]).then_inc(dve_setup, 1)
            eng.wait_ge(dve_setup, 3)

            def att_stats(n, m, p):
                eng.wait_ge(x_loaded[p], 32 * (m + 1))
                ve_.bn_stats(st6[:, 0, :], xc[:, p, :])
                ve_.bn_stats(st6[:, 1, :], xs[:, p, :]).then_inc(dve_att.sem, 1)
                v0 = held(eng, regs[0], dve_att.count("stats", n))
                eng.wait_ge(dve_setup, 3)
                eng.wait_ge(dve_att.sem, v0)
                ve_.bn_aggr(mv[:, 0, :], st6[:, 0, :])
                ve_.bn_aggr(mv[:, 1, :], st6[:, 1, :]).then_inc(dve_att.sem, 1)

            def att_norm(n, m, p):
                eng.wait_ge(pool_att.sem, pool_att.count("rstd", n))
                eng.wait_ge(dve_att.sem, dve_att.count("aggr", n))
                eng.wait_ge(pe_att.sem, pe_att.count("T3", n - 1))
                ve_.tensor_scalar(xn, xc[:, p, :], mv[:, 0, 0:1], rstd[:, 0:1],
                                  ALU.subtract, ALU.mult).then_inc(dve_att.sem, 1)
                ve_.tensor_scalar(yn, xs[:, p, :], mv[:, 1, 0:1], rstd[:, 1:2],
                                  ALU.subtract, ALU.mult).then_inc(dve_att.sem, 1)

            def att_v(n, m, p):
                eng.wait_ge(pe_att.sem, pe_att.count("V", n))
                ve_.tensor_tensor(v_att[:, :, :], by_chunk(bank_of("V")[:, :]),
                                  vbias[:, :].unsqueeze(1).broadcast_to([P, C, P]),
                                  ALU.add).then_inc(dve_att.sem, 1)

            def att_max(n, m, p, t):
                eng.wait_ge(pe_att.sem, pe_att.count(f"S{t}", n))
                ve_.tensor_reduce(nmax[:, t:t + 1], bank_of(f"S{t}")[:, :], X, ALU.max,
                                  negate=True).then_inc(dve_att.sem, 1)

            def att_rinv(n, m, p, t):
                eng.wait_ge(act_att.sem, act_att.count(f"p{t}", n))
                ve_.reciprocal(rinv[:, t:t + 1], rsum[:, t:t + 1]).then_inc(dve_att.sem, 1)

            def att_xin(n, m, p):
                eng.wait_ge(pe_att.sem, pe_att.count("O", n))
                eng.wait_ge(pool_mid.sem, pool_mid.count("xres", n - 2))
                ve_.scalar_tensor_tensor(xin[:, p, :], bank_of("O")[:, :], col("bo", 0), xc[:, p, :],
                                         ALU.add, ALU.add).then_inc(dve_att.sem, 1)
                eng.wait_ge(dve_att.sem, dve_att.count("xin", n))
                ve_.bn_stats(st6[:, 2, :], xin[:, p, :]).then_inc(dve_att.sem, 1)
                v0 = held(eng, regs[0], dve_att.count("xst", n))
                eng.wait_ge(dve_setup, 3)
                eng.wait_ge(dve_att.sem, v0)
                ve_.bn_aggr(mv[:, 2, :], st6[:, 2, :]).then_inc(dve_att.sem, 1)

            def att_xhat(n, m, p):
                eng.wait_ge(pool_att.sem, pool_att.count("rstd1", n))
                eng.wait_ge(pe_mid.sem, pe_mid.count("Tx", n - 1))
                ve_.tensor_scalar(xhat[:, :], xin[:, p, :], mv[:, 2, 0:1], rstd[:, 2:3],
                                  ALU.subtract, ALU.mult).then_inc(dve_att.sem, 1)

            def mid_shift(n, m, p):
                eng.wait_ge(act_mid.sem, act_mid.count("xa", n))
                eng.wait_ge(pool_mid.sem, pool_mid.count("xa0", n))
                ve_.tensor_tensor(sx[:, :, :], xa[:, :, 0:P], xa[:, :, 1:P + 1],
                                  ALU.subtract).then_inc(dve_mid.sem, 1)
                eng.wait_ge(dve_mid.sem, dve_mid.count("sx", n))
                eng.wait_ge(pe_mid.sem, pe_mid.count("W1", n - 1))
                for c in range(C):
                    last = ve_.scalar_tensor_tensor(xx[:, c, :], sx[:, c, :], col("maa_x", c), xa[:, c, 1:P + 1],
                                                    ALU.mult, ALU.add)
                last.then_inc(dve_mid.sem, 1)

            def mid_mix(n, m, p, i):
                f, b = ORDER[i], i % 2
                before = ORDER[i - 2] if i >= 2 else {0: "g", 1: "r"}[i]
                eng.wait_ge(pe_mid.sem, pe_mid.count(f"M{f}", n))
                eng.wait_ge(pool_mid.sem, pool_mid.count(f"f{before}", n if i >= 2 else n - 1))
                ps = bank_of(f"M{f}")
                for c in range(C):
                    last = ve_.scalar_tensor_tensor(mt[:, b, c, :], ps[:, c * P:(c + 1) * P],
                                                    col("maa_stack", c, MIX.index(f)), sx[:, c, :], ALU.add, ALU.mult)
                last.then_inc(dve_mid.sem, 1)

            def mid_gate(n, m, p):
                eng.wait_ge(act_mid.sem, act_mid.count("th", n))
                eng.wait_ge(pool_tail.sem, pool_tail.count("gb", n - 2))
                ve_.scalar_tensor_tensor(gN[:, p, :], th[:, :], 1.0, bank_of("G")[:, :],
                                         ALU.add, ALU.mult).then_inc(dve_mid.sem, 1)

            def wkv_outer(n, m, p, u):
                eng.wait_ge(vrep_loaded[u % 2], 16 * (n * (U // 2) + u // 2 + 1))
                if u == 0:
                    eng.wait_ge(act_mid.sem, act_mid.count("k", n))
                v = vrep[:, u % 2, :, :]
                ve_.tensor_tensor(v, v, kT[:, p, u // 2, :].unsqueeze(1).broadcast_to([P, UJ, P]),
                                  ALU.mult).then_inc(dve_wkv.sem, 1)

            def wkv_scan(n, m, p, u):
                eng.wait_ge(dve_wkv.sem, dve_wkv.count(f"a{u}", n))
                if u == 0:
                    eng.wait_ge(act_mid.sem, act_mid.count("w", n))
                    eng.wait_ge(s0_loaded[p], 16 * (m + 1))
                eng.wait_ge(pe_wkv.sem, pe_wkv.count(f"r{(u - 2) % U}", n if u >= 2 else n - 1))
                for j in range(UJ):
                    k = UJ * u + j
                    last = ve_.tensor_tensor_scan(S[:, u % 2, j, 1:P], wT[:, p, u // 2, 0:P - 1],
                                                  vrep[:, u % 2, j, 0:P - 1], s0[:, p, k:k + 1], ALU.mult, ALU.add)
                last.then_inc(dve_wkv.sem, 1)

            def wkv_read(n, m, p, u):
                eng.wait_ge(dve_wkv.sem, dve_wkv.count(f"s{u}", n))
                eng.wait_ge(pool_wkv.sem, pool_wkv.count(f"z{u}", n))
                if u == 0:
                    eng.wait_ge(act_mid.sem, act_mid.count("r", n))
                s = S[:, u % 2, :, :]
                ve_.tensor_tensor(s, s, rT[:, p, u // 2, :].unsqueeze(1).broadcast_to([P, UJ, P]),
                                  ALU.mult).then_inc(dve_wkv.sem, 1)

            def heads(ap):
                return ap.rearrange("p (h j) -> p h j", j=HS)

            def over_head(ap):
                return ap.unsqueeze(2).broadcast_to([P, H, HS])

            def tail_o(n, m, p):
                eng.wait_ge(pe_tail.sem, pe_tail.count("C", n))
                eng.wait_ge(pe_tail.sem, pe_tail.count("To", n - 1))
                ve_.tensor_tensor(og[:, :], vT[:, p, :, :].rearrange("p c t -> p (c t)"), bank_of("C")[:, :],
                                  ALU.mult).then_inc(dve_tail.sem, 1)
                eng.wait_ge(dve_tail.sem, dve_tail.count("o1", n))
                eng.wait_ge(pe_wkv.sem, pe_wkv.count(f"r{U - 1}", n))
                ve_.tensor_tensor(og[:, :], og[:, :], bank[WKV_BANKS[p]][:, :], ALU.add).then_inc(dve_tail.sem, 1)

            def tail_mean(n, m, p):
                eng.wait_ge(pe_tail.sem, pe_tail.count("To", n))
                o = heads(bank_of("To")[:, :])
                ve_.tensor_reduce(hsum[:, 0, :], o, X, ALU.add).then_inc(dve_tail.sem, 1)
                eng.wait_ge(dve_tail.sem, dve_tail.count("sum", n))
                eng.wait_ge(pe_tail.sem, pe_tail.count("Tg", n - 1))
                ve_.scalar_tensor_tensor(heads(oc[:, :]), over_head(hsum[:, 0, :]), -1.0 / HS, o,
                                         ALU.mult, ALU.add).then_inc(dve_tail.sem, 1)

            def tail_var(n, m, p):
                eng.wait_ge(pool_tail.sem, pool_tail.count("sq", n))
                ve_.tensor_reduce(hsum[:, 1, :], heads(sq[:, :]), X, ALU.add).then_inc(dve_tail.sem, 1)

            def tail_gn(n, m, p):
                eng.wait_ge(pool_tail.sem, pool_tail.count("hrs", n))
                ve_.tensor_tensor(heads(oc[:, :]), heads(oc[:, :]), over_head(hrs[:, :]),
                                  ALU.mult).then_inc(dve_tail.sem, 1)
                eng.wait_ge(dve_tail.sem, dve_tail.count("o3", n))
                ve_.tensor_tensor(oc[:, :], oc[:, :], gw[:, :], ALU.mult).then_inc(dve_tail.sem, 1)
                eng.wait_ge(dve_tail.sem, dve_tail.count("o4", n))
                ve_.tensor_tensor(oc[:, :], oc[:, :], gb[:, :], ALU.add).then_inc(dve_tail.sem, 1)

            def tail_x1(n, m, p):
                eng.wait_ge(pe_tail.sem, pe_tail.count("Wo", n))
                eng.wait_ge(pool_mid.sem, pool_mid.count("xres", n))
                eng.wait_ge(pool_fin.sem, pool_fin.count("out", n - 1))
                ve_.tensor_tensor(x1[:, :], bank_of("Wo")[:, :], xres[:, p, :], ALU.add).then_inc(dve_tail.sem, 1)
                eng.wait_ge(dve_tail.sem, dve_tail.count("x1", n))
                ve_.bn_stats(st62[:, :], x1[:, :]).then_inc(dve_tail.sem, 1)
                v0 = held(eng, regs[0], dve_tail.count("st", n))
                eng.wait_ge(dve_setup, 3)
                eng.wait_ge(dve_tail.sem, v0)
                ve_.bn_aggr(mv2[:, :], st62[:, :]).then_inc(dve_tail.sem, 1)

            def tail_xhat(n, m, p):
                eng.wait_ge(pool_tail.sem, pool_tail.count("rstd2", n))
                ve_.tensor_scalar(xhat2[:, :], x1[:, :], mv2[:, 0:1], rstd2[:, 0:1],
                                  ALU.subtract, ALU.mult).then_inc(dve_tail.sem, 1)

            def tail_shift(n, m, p):
                eng.wait_ge(act_tail.sem, act_tail.count("xc2", n))
                eng.wait_ge(pool_tail.sem, pool_tail.count("xc20", n))
                ve_.tensor_tensor(sx2[:, :, :], xc2[:, :, 0:P], xc2[:, :, 1:P + 1],
                                  ALU.subtract).then_inc(dve_tail.sem, 1)
                eng.wait_ge(dve_tail.sem, dve_tail.count("sx2", n))
                eng.wait_ge(pe_fin.sem, pe_fin.count("FR", n - 1))
                for dst, mix in ((xk2, "ffn_maa_k"), (xr2, "ffn_maa_r")):
                    for c in range(C):
                        last = ve_.scalar_tensor_tensor(dst[:, c, :], sx2[:, c, :], col(mix, c), xc2[:, c, 1:P + 1],
                                                        ALU.mult, ALU.add)
                    last.then_inc(dve_tail.sem, 1)

            def fin_y(n, m, p):
                eng.wait_ge(act_fin.sem, act_fin.count("rr", n))
                eng.wait_ge(pe_fin.sem, pe_fin.count("FV", n))
                ve_.tensor_tensor(rr[:, :], bank_of("FV")[:, :], rr[:, :], ALU.mult).then_inc(dve_fin.sem, 1)

            def step(s, on):
                a, m, w, t, f = (on.get(k) for k in LAG)

                if w: wkv_outer(*w, 0)
                if t: tail_o(*t)
                if w: wkv_scan(*w, 0)
                if a: att_stats(*a)
                if w: wkv_read(*w, 0)

                if a: att_norm(*a)
                if m: mid_shift(*m)
                if w: wkv_outer(*w, 1)
                if w: wkv_scan(*w, 1)
                if t: tail_mean(*t)
                if w: wkv_read(*w, 1)

                if w: wkv_outer(*w, 2)
                if a: att_v(*a)
                if w: wkv_scan(*w, 2)
                if t: tail_var(*t)
                if w: wkv_read(*w, 2)
                if a: att_max(*a, 0)
                if m: mid_mix(*m, 0)

                if w: wkv_outer(*w, 3)
                if a: att_max(*a, 1)
                if a: att_rinv(*a, 0)
                if m: mid_mix(*m, 1)
                if w: wkv_scan(*w, 3)
                if a: att_rinv(*a, 1)
                if a: att_max(*a, 2)
                if f: fin_y(*f)
                if w: wkv_read(*w, 3)

                if w: wkv_outer(*w, 4)
                if m: mid_mix(*m, 2)
                if a: att_max(*a, 3)
                if w: wkv_scan(*w, 4)
                if a: att_rinv(*a, 2)
                if a: att_rinv(*a, 3)
                if t: tail_gn(*t)
                if w: wkv_read(*w, 4)

                if w: wkv_outer(*w, 5)
                if m: mid_mix(*m, 3)
                if w: wkv_scan(*w, 5)
                if w: wkv_read(*w, 5)

                if t: tail_x1(*t)
                if w: wkv_outer(*w, 6)
                if m: mid_mix(*m, 4)
                if w: wkv_scan(*w, 6)
                if t: tail_xhat(*t)
                if w: wkv_read(*w, 6)

                if w: wkv_outer(*w, 7)
                if w: wkv_scan(*w, 7)
                if t: tail_shift(*t)
                if w: wkv_read(*w, 7)
                if a: att_xin(*a)
                if m: mid_gate(*m)
                if a: att_xhat(*a)

            run(eng, step)

        @block.scalar
        def _(eng):
            sc = nc.scalar
            eng.wait_ge(setup_loaded[0], 32)

            def att_proj(n, m, p):
                for job, dst, bias in (("Mn", Mn, "bn"), ("Mm", Mm, "bm")):
                    eng.wait_ge(pe_att.sem, pe_att.count(job, n))
                    sc.activation(dst[:, :], bank_of(job)[:, :], ACT.Identity,
                                  bias=col(bias, 0)).then_inc(act_att.sem, 1)

            def att_exp(n, m, p, t):
                eng.wait_ge(dve_att.sem, dve_att.count(f"mx{t}", n))
                sc.activation(prob[:, t, :], bank_of(f"S{t}")[:, :], ACT.Exp, bias=nmax[:, t:t + 1],
                              accum_out=rsum[:, t:t + 1]).then_inc(act_att.sem, 1)

            def att_scale(n, m, p, t):
                eng.wait_ge(dve_att.sem, dve_att.count(f"ri{t}", n))
                sc.activation(prob[:, t, :], prob[:, t, :], ACT.Identity,
                              scale=rinv[:, t:t + 1]).then_inc(act_att.sem, 1)

            def att_probT(n, m, p, c):
                eng.wait_ge(pe_att.sem, pe_att.count(f"T{c}", n))
                eng.wait_ge(pe_att.sem, pe_att.count("O", n - 1))
                sc.activation(probT[:, c, :], bank_of(f"T{c}")[:, :], ACT.Copy).then_inc(act_att.sem, 1)

            def mid_xa(n, m, p):
                eng.wait_ge(pe_mid.sem, pe_mid.count("Tx", n))
                eng.wait_ge(dve_mid.sem, dve_mid.count("xx", n - 1))
                eng.wait_ge(pool_mid.sem, pool_mid.count("fg", n - 1))
                for c in range(C):
                    last = sc.activation(xa[:, c, 1:P + 1], bank_of("Tx")[:, c * P:(c + 1) * P], ACT.Identity,
                                         bias=col("ln1_b", c), scale=col("ln1_w", c))
                last.then_inc(act_mid.sem, 1)

            def mid_tx(n, m, p):
                eng.wait_ge(pe_mid.sem, pe_mid.count("W1", n))
                sc.activation(tx[:, :], bank_of("W1")[:, 0:P], ACT.Tanh)
                sc.activation(txg[:, :], bank_of("W1")[0:DM, P:2 * P], ACT.Tanh).then_inc(act_mid.sem, 1)

            def mid_v(n, m, p):
                eng.wait_ge(pe_mid.sem, pe_mid.count("Vp", n))
                eng.wait_ge(dve_tail.sem, dve_tail.count("o1", n - 2))
                eng.wait_ge(v_stored, 16 * (n - 1) if not isinstance(n, int) or n > 0 else 0)
                sc.activation(vT[:, p, :, :], by_chunk(bank_of("Vp")[:, :]), ACT.Copy).then_inc(act_mid.sem, 1)
                eng.wait_ge(act_mid.sem, act_mid.count("vT", n))
                eng.wait_ge(dve_wkv.sem, dve_wkv.count(f"a{U - 1}", n - 2))
                eng.dma_start(v_dram[p].rearrange("(c e) t -> e c t", c=C), vT[:, p, :, :]).then_inc(v_stored, 16)

            def mid_dt(n, m, p):
                eng.wait_ge(pe_mid.sem, pe_mid.count("D1", n))
                sc.activation(dt[:, :], bank_of("D1")[0:DD, 0:P], ACT.Tanh).then_inc(act_mid.sem, 1)

            def mid_k(n, m, p):
                eng.wait_ge(pe_mid.sem, pe_mid.count("Kp", n))
                sc.activation(kT[:, p, :, :], by_chunk(bank_of("Kp")[:, :]), ACT.Copy).then_inc(act_mid.sem, 1)

            def mid_w(n, m, p):
                eng.wait_ge(pe_mid.sem, pe_mid.count("D2", n))
                for c in range(C):
                    last = sc.activation(ez[:, c, :], bank_of("D2")[:, c * P:(c + 1) * P], ACT.Exp,
                                         bias=col("time_decay", c))
                last.then_inc(act_mid.sem, 1)
                eng.wait_ge(act_mid.sem, act_mid.count("ez", n))
                sc.activation(wT[:, p, :, :], ez[:, :, :], ACT.Exp, scale=-1.0).then_inc(act_mid.sem, 1)

            def mid_r(n, m, p):
                eng.wait_ge(pe_mid.sem, pe_mid.count("Rp", n))
                sc.activation(rT[:, p, :, :], by_chunk(bank_of("Rp")[:, :]), ACT.Copy).then_inc(act_mid.sem, 1)

            def mid_th(n, m, p):
                eng.wait_ge(pe_mid.sem, pe_mid.count("G", n))
                sc.activation(th[:, :], bank_of("G")[:, :], ACT.Tanh, scale=0.5).then_inc(act_mid.sem, 1)

            def tail_oT(n, m, p):
                eng.wait_ge(pe_tail.sem, pe_tail.count("Tg", n))
                sc.activation(ogT[:, :, :], by_chunk(bank_of("Tg")[:, :]), ACT.Copy).then_inc(act_tail.sem, 1)

            def tail_xc2(n, m, p):
                eng.wait_ge(pe_tail.sem, pe_tail.count("Tx2", n))
                eng.wait_ge(dve_tail.sem, dve_tail.count("xr2", n - 1))
                for c in range(C):
                    last = sc.activation(xc2[:, c, 1:P + 1], bank_of("Tx2")[:, c * P:(c + 1) * P], ACT.Identity,
                                         bias=col("ln2_b", c), scale=col("ln2_w", c))
                last.then_inc(act_tail.sem, 1)

            def fin_kr(n, m, p):
                eng.wait_ge(pe_tail.sem, pe_tail.count("FK", n))
                eng.wait_ge(pe_fin.sem, pe_fin.count("FV", n - 1))
                sc.activation(kk[:, :, :], by_chunk(bank_of("FK")[:, :]), ACT.Relu).then_inc(act_fin.sem, 1)

            def fin_rr(n, m, p):
                eng.wait_ge(pe_fin.sem, pe_fin.count("FR", n))
                eng.wait_ge(out_stored, 16 * n)
                sc.activation(rr[:, :], bank_of("FR")[:, :], ACT.Tanh, scale=0.5).then_inc(act_fin.sem, 1)
                eng.wait_ge(act_fin.sem, act_fin.count("thr", n))
                sc.activation(rr[:, :], rr[:, :], ACT.Copy, bias=0.5, scale=0.5).then_inc(act_fin.sem, 1)

            def fin_store(n, m, p):
                eng.wait_ge(pool_fin.sem, pool_fin.count("out", n))
                dst = out[n] if isinstance(n, int) else out[bass.ds(n, 1)].rearrange("o p f -> (o p) f")
                eng.dma_start(dst, rr[:, :]).then_inc(out_stored, 16)

            def step(s, on):
                a, m, w, t, f = (on.get(k) for k in LAG)
                if f: fin_kr(*f)
                if m: mid_xa(*m)
                if f: fin_rr(*f)
                if a: att_proj(*a)
                if m: mid_tx(*m)
                if a: att_exp(*a, 0)
                if a: att_exp(*a, 1)
                if a: att_scale(*a, 0)
                if a: att_scale(*a, 1)
                if a: att_exp(*a, 2)
                if m: mid_v(*m)
                if f: fin_store(*f)
                if a: att_exp(*a, 3)
                if a: att_scale(*a, 2)
                if a: att_scale(*a, 3)
                if m: mid_dt(*m)
                if m: mid_k(*m)
                if t: tail_oT(*t)
                if m: mid_w(*m)
                for c in range(C):
                    if a: att_probT(*a, c)
                if m: mid_r(*m)
                if t: tail_xc2(*t)
                if m: mid_th(*m)

            run(eng, step)
            eng.wait_ge(out_stored, 16 * NB)

        @block.tensor
        def _(eng):
            pe = nc.tensor
            eng.wait_ge(setup_loaded[0], 32)
            pe.matmul(bank[0][:, 0:P], attw[:, 2, :], attw[:, 3, :], start=True, stop=True).then_inc(pe_setup, 1)
            eng.wait_ge(dve_setup, 1)
            pe.matmul(bank[1][:, 0:P], bl_rep, attw[:, 3, :], start=True, stop=True).then_inc(pe_setup, 1)
            eng.wait_ge(dve_setup, 3)
            eng.wait_ge(pool_const, 9)

            def proj_T(job, w, src):
                ps = bank_of(job)
                for o in range(C):
                    for c in range(C):
                        last = pe.matmul(ps[:, o * P:(o + 1) * P], w[:, c, o * P:(o + 1) * P], src[:, c, :],
                                         start=(c == 0), stop=(c == C - 1))
                return last

            def proj_N(job, w, src):
                for c in range(C):
                    last = pe.matmul(bank_of(job)[:, :], src[:, c, :], w[:, c, :], start=(c == 0), stop=(c == C - 1))
                return last

            def transposes(job, src):
                for c in range(C):
                    last = pe.transpose(bank_of(job)[:, c * P:(c + 1) * P], src(c), ident[:, :])
                return last

            def att_M(n, m, p):
                eng.wait_ge(dve_att.sem, dve_att.count("xn", n))
                eng.wait_ge(*bank_free("Mn", n))
                pe.matmul(bank_of("Mn")[:, :], attw[:, 0, :], xn, start=True, stop=True).then_inc(pe_att.sem, 1)
                eng.wait_ge(dve_att.sem, dve_att.count("yn", n))
                eng.wait_ge(*bank_free("Mm", n))
                pe.matmul(bank_of("Mm")[:, :], attw[:, 1, :], yn, start=True, stop=True).then_inc(pe_att.sem, 1)

            def att_V(n, m, p):
                eng.wait_ge(*bank_free("V", n))
                for c in range(C):
                    last = pe.matmul(bank_of("V")[:, c * P:(c + 1) * P], xs[:, p, c * P:(c + 1) * P], wolT[:, :],
                                     start=True, stop=True)
                last.then_inc(pe_att.sem, 1)

            def att_S(n, m, p, t):
                eng.wait_ge(act_att.sem, act_att.count("Mm", n))
                eng.wait_ge(*bank_free(f"S{t}", n))
                pe.matmul(bank_of(f"S{t}")[:, :], Mn[:, t * P:(t + 1) * P], Mm[:, :],
                          start=True, stop=True).then_inc(pe_att.sem, 1)

            def att_T(n, m, p):
                eng.wait_ge(act_att.sem, act_att.count("n3", n))
                for c in range(C):
                    eng.wait_ge(*bank_free(f"T{c}", n))
                    transposes(f"T{c}", lambda t: prob[:, t, c * P:(c + 1) * P]).then_inc(pe_att.sem, 1)

            def att_O(n, m, p):
                eng.wait_ge(*bank_free("O", n))
                eng.wait_ge(dve_att.sem, dve_att.count("vatt", n))
                for c in range(C):
                    eng.wait_ge(act_att.sem, act_att.count(f"T{c}", n))
                    last = pe.matmul(bank_of("O")[:, :], v_att[:, c, :], probT[:, c, :],
                                     start=(c == 0), stop=(c == C - 1))
                last.then_inc(pe_att.sem, 1)

            def mid_Tx(n, m, p):
                eng.wait_ge(dve_att.sem, dve_att.count("xhat", n))
                eng.wait_ge(*bank_free("Tx", n))
                transposes("Tx", lambda c: xhat[:, c * P:(c + 1) * P]).then_inc(pe_mid.sem, 1)

            def mid_W1(n, m, p):
                if isinstance(n, int) and n == 0:
                    eng.wait_ge(setup_loaded[1], 80)
                eng.wait_ge(dve_mid.sem, dve_mid.count("xx", n))
                eng.wait_ge(*bank_free("W1", n))
                ps = bank_of("W1")
                for c in range(C):
                    pe.matmul(ps[:, 0:P], w1[:, c, 0:P], xx[:, c, :], start=(c == 0), stop=(c == C - 1))
                for c in range(C):
                    last = pe.matmul(ps[0:DM, P:2 * P], w1[:, c, P:P + DM], xx[:, c, :],
                                     start=(c == 0), stop=(c == C - 1))
                last.then_inc(pe_mid.sem, 1)

            def mid_M(n, m, p, f):
                i = MIX.index(f)
                eng.wait_ge(act_mid.sem, act_mid.count("tx", n))
                eng.wait_ge(*bank_free(f"M{f}", n))
                w, x_ = (w2g[:, :], txg[:, :]) if f == "g" else (w2[DM * i:DM * i + DM, :], tx[DM * i:DM * i + DM, :])
                for c in range(C):
                    last = pe.matmul(bank_of(f"M{f}")[:, c * P:(c + 1) * P], w[:, c * P:(c + 1) * P], x_,
                                     start=True, stop=True)
                last.then_inc(pe_mid.sem, 1)

            def xf_of(f):
                return xf[:, ORDER.index(f) % 2, :, :]

            def mid_P(n, m, p, f, job, name):
                if isinstance(n, int) and n == 0:
                    eng.wait_ge(setup_loaded[2], 16 * len(BIG))
                eng.wait_ge(pool_mid.sem, pool_mid.count(f"f{f}", n))
                eng.wait_ge(*bank_free(job, n))
                if f == "g":
                    proj_N(job, W[name], xf_of(f)).then_inc(pe_mid.sem, 1)
                else:
                    proj_T(job, W[name], xf_of(f)).then_inc(pe_mid.sem, 1)

            def mid_D1(n, m, p):
                eng.wait_ge(pool_mid.sem, pool_mid.count("fw", n))
                eng.wait_ge(*bank_free("D1", n))
                for c in range(C):
                    last = pe.matmul(bank_of("D1")[0:DD, 0:P], tw1[:, c, :], xf_of("w")[:, c, :],
                                     start=(c == 0), stop=(c == C - 1))
                last.then_inc(pe_mid.sem, 1)

            def mid_D2(n, m, p):
                eng.wait_ge(act_mid.sem, act_mid.count("dt", n))
                eng.wait_ge(*bank_free("D2", n))
                for c in range(C):
                    last = pe.matmul(bank_of("D2")[:, c * P:(c + 1) * P], tw2[:, c * P:(c + 1) * P], dt[:, :],
                                     start=True, stop=True)
                last.then_inc(pe_mid.sem, 1)

            def wkv_sum(n, m, p, u):
                eng.wait_ge(dve_wkv.sem, dve_wkv.count(f"q{u}", n))
                if u == 0:
                    eng.wait_ge(dve_tail.sem, dve_tail.count("o2", n - 2))
                o = bank[WKV_BANKS[p]][:, u // 2 * P:(u // 2 + 1) * P]
                for jj in range(UJ):
                    j = UJ * (u % 2) + jj
                    last = pe.matmul(o, slide[:, HS - 1 - j:HS - 1 - j + P], S[:, u % 2, jj, :],
                                     start=(j == 0), stop=(j == HS - 1))
                last.then_inc(pe_wkv.sem, 1)

            def tail_C(n, m, p):
                eng.wait_ge(pool_wkv.sem, pool_wkv.count("rku", n))
                eng.wait_ge(*bank_free("C", n))
                pe.matmul(bank_of("C")[:, :], head_rep[:, :], rku[:, :, :].rearrange("p c t -> p (c t)"),
                          start=True, stop=True).then_inc(pe_tail.sem, 1)

            def tail_To(n, m, p):
                eng.wait_ge(dve_tail.sem, dve_tail.count("o2", n))
                eng.wait_ge(*bank_free("To", n))
                transposes("To", lambda c: og[:, c * P:(c + 1) * P]).then_inc(pe_tail.sem, 1)

            def tail_Tg(n, m, p):
                eng.wait_ge(dve_tail.sem, dve_tail.count("o5", n))
                eng.wait_ge(*bank_free("Tg", n))
                transposes("Tg", lambda c: oc[:, c * P:(c + 1) * P]).then_inc(pe_tail.sem, 1)

            def tail_Wo(n, m, p):
                eng.wait_ge(act_tail.sem, act_tail.count("oT", n))
                eng.wait_ge(*bank_free("Wo", n))
                proj_N("Wo", W["Wo"], ogT).then_inc(pe_tail.sem, 1)

            def tail_Tx2(n, m, p):
                eng.wait_ge(dve_tail.sem, dve_tail.count("xh", n))
                eng.wait_ge(*bank_free("Tx2", n))
                transposes("Tx2", lambda c: xhat2[:, c * P:(c + 1) * P]).then_inc(pe_tail.sem, 1)

            def tail_FK(n, m, p):
                eng.wait_ge(dve_tail.sem, dve_tail.count("xk2", n))
                eng.wait_ge(*bank_free("FK", n))
                proj_T("FK", W["Wfk"], xk2).then_inc(pe_tail.sem, 1)

            def fin_FR(n, m, p):
                eng.wait_ge(dve_tail.sem, dve_tail.count("xr2", n))
                eng.wait_ge(*bank_free("FR", n))
                proj_N("FR", W["Wfr"], xr2).then_inc(pe_fin.sem, 1)

            def fin_FV(n, m, p):
                eng.wait_ge(pool_fin.sem, pool_fin.count("kk", n))
                eng.wait_ge(*bank_free("FV", n))
                proj_N("FV", W["Wfv"], kk).then_inc(pe_fin.sem, 1)

            def step(s, on):
                a, m, w, t, f = (on.get(k) for k in LAG)

                if m: mid_Tx(*m)
                if t: tail_C(*t)
                if f: fin_FR(*f)
                if w: wkv_sum(*w, 0)

                if a: att_M(*a)
                if a: att_V(*a)
                if t: tail_To(*t)
                if f: fin_FV(*f)
                if w: wkv_sum(*w, 1)

                if m: mid_W1(*m)
                if a: att_S(*a, 0)
                if a: att_S(*a, 1)
                if m: mid_M(*m, "v")
                if w: wkv_sum(*w, 2)

                if m: mid_M(*m, "w")
                if a: att_S(*a, 2)
                if a: att_S(*a, 3)
                if m: mid_M(*m, "k")
                if m: mid_P(*m, "v", "Vp", "Wv")
                if w: wkv_sum(*w, 3)

                if m: mid_D1(*m)
                if m: mid_P(*m, "k", "Kp", "Wk")
                if t: tail_Tg(*t)
                if m: mid_M(*m, "r")
                if w: wkv_sum(*w, 4)

                if m: mid_D2(*m)
                if t: tail_Wo(*t)
                if a: att_T(*a)
                if m: mid_M(*m, "g")
                if w: wkv_sum(*w, 5)

                if m: mid_P(*m, "r", "Rp", "Wr")
                if t: tail_Tx2(*t)
                if a: att_O(*a)
                if w: wkv_sum(*w, 6)

                if m: mid_P(*m, "g", "G", "Wg")
                if t: tail_FK(*t)
                if w: wkv_sum(*w, 7)

            run(eng, step)


def kernel(**inputs):
    import numpy as np
    import concourse.bacc as bacc
    from concourse.bass_utils import run_bass_kernel_spmd

    a = {k.replace("_xattn_", "_"): np.asarray(v) for k, v in inputs.items()}

    def chunked(w):
        return np.ascontiguousarray(w.reshape(C, P, -1).transpose(1, 0, 2))

    def column(v):
        return v.reshape(C, P).T

    ctx = a["ctx_2048"]
    one = lambda v: v.reshape(P, 1)
    u = a["L1_u"].reshape(E)
    params = np.concatenate(
        [column(a["L1_" + k]) for k in ("ln1_w", "ln1_b", "ln2_w", "ln2_b", "maa_x", "time_decay",
                                         "ffn_maa_k", "ffn_maa_r")]
        + [column(u)] + [column(a["L1_maa_stack"][0, f]) for f in range(5)]
        + [one(a["L0_" + k]) for k in ("bn", "bm", "bl", "bo")], axis=1)
    rows = ctx[:, 0:2, :].reshape(NB, 2, C, P).transpose(0, 3, 1, 2).reshape(NB, P, 2 * C)
    s0 = ctx[:, 2:2 + HS, :].reshape(NB, C, P, HS).transpose(0, 2, 1, 3).reshape(NB, P, C * HS)
    arrays = {
        "x_c": a["x"],
        "x_s": ctx,
        "state": np.concatenate([rows, s0], axis=2),
        "params": params,
        "att_w": np.stack([a["L0_Wn"].T, a["L0_Wm"].T, a["L0_Wl"], a["L0_Wo"].T], axis=1),
        "big_w": np.stack([chunked(a["L1_" + k].T) for k in BIG]),
        "maa_w1": chunked(a["L1_maa_w1"]),
        "maa_w2": a["L1_maa_w2"].reshape(5 * DM, E),
        "td_w1": chunked(a["L1_td_w1"]),
        "td_w2": a["L1_td_w2"],
        "gn": np.stack([a["L1_gn_w"], a["L1_gn_b"]]),
    }
    arrays = {k: np.ascontiguousarray(v) for k, v in arrays.items()}
    nc = bacc.Bacc("TRN2", target_bir_lowering=False, num_devices=1)
    args = [nc.dram_tensor(k, v.shape, mybir.dt.from_np(v.dtype), kind="ExternalInput").ap()
            for k, v in arrays.items()]
    args.append(nc.dram_tensor("out", (NB, P, E), F32, kind="ExternalOutput").ap())
    args.append(nc.dram_tensor("v_dram", (2, E, P), F32).ap())
    build(nc, *args)
    result = run_bass_kernel_spmd(nc, [arrays], core_ids=[0])
    return result.results[0]["out"]
```
